# Optimizing a Trainium2 kernel written in Bass

```python
import numpy as np
import jax
import jax.numpy as jnp

def _softmax(x, axis=-1):
    return jax.nn.softmax(x, axis=axis)

def _gelu(x):
    return jax.nn.gelu(x, approximate=True)

def _silu(x):
    return jax.nn.silu(x)

def _sigmoid(x):
    return jax.nn.sigmoid(x)

def _layernorm(x, axis=-1, eps=1e-05):
    m = jnp.mean(x, axis=axis, keepdims=True)
    v = jnp.var(x, axis=axis, keepdims=True)
    return (x - m) / jnp.sqrt(v + eps)

def _scatter_add(tgt, idx, src, axis=0):
    return tgt.at[idx].add(src)

def _segment_sum(src, seg, n):
    return jax.ops.segment_sum(src, seg, n)
kernel_name = 'mk_conv_seq_d2_conv_nchw512_r2_19dfc5'

def setup_inputs(seed: int=0):
    np.random.seed(seed)
    _w = jnp.asarray

    def _rec_inputs():
        import jax
        import jax.numpy as jnp
        _gk = jax.random.key(seed)
        x = 7.22e-05 + 1 * jax.random.normal(jax.random.fold_in(_gk, 1), (16, 256, 32, 32), jnp.float32)
        return x
    x = _rec_inputs()

    def _L0_conv_setup():
        import math
        import jax, jax.numpy as jnp
        import numpy as np
        CH = 256
        NUM_HEADS = 4
        GROUPS = 32
        EPS = 1e-05

        def group_norm(x, gamma, beta):
            b, c, h, w = x.shape
            xg = x.reshape(b, GROUPS, c // GROUPS, h * w)
            mean = jnp.mean(xg, axis=(2, 3), keepdims=True)
            var = jnp.var(xg, axis=(2, 3), keepdims=True)
            xn = (xg - mean) * jax.lax.rsqrt(var + EPS)
            xn = xn.reshape(b, c, h, w)
            return xn * gamma[None, :, None, None] + beta[None, :, None, None]
        key = jax.random.key(seed)
        ks = jax.random.split(key, 3)
        x = jax.random.normal(ks[0], (16, CH, 32, 32), dtype=jnp.float32)
        qkv_w = jax.random.normal(ks[1], (3 * CH, CH), dtype=jnp.float32) * (1.0 / math.sqrt(CH))
        qkv_b = jnp.zeros((3 * CH,), dtype=jnp.float32)
        proj_w = jax.random.normal(ks[2], (CH, CH), dtype=jnp.float32) * (1.0 / math.sqrt(CH))
        proj_b = jnp.zeros((CH,), dtype=jnp.float32)
        gn_w = jnp.ones((CH,), dtype=jnp.float32)
        gn_b = jnp.zeros((CH,), dtype=jnp.float32)
        return {'x': x, 'gn_w': gn_w, 'gn_b': gn_b, 'qkv_w': qkv_w, 'qkv_b': qkv_b, 'proj_w': proj_w, 'proj_b': proj_b}
    _L0_conv_all = _L0_conv_setup()
    _L0_conv_in = {k: v for k, v in _L0_conv_all.items() if k in ('gn_w', 'gn_b', 'qkv_w', 'qkv_b', 'proj_w', 'proj_b')}
    del _L0_conv_all

    def _L1_conv_setup():
        import jax, jax.numpy as jnp
        import numpy as np
        from jax import lax
        EPS = 1e-05

        def _bn(x, g, b, m, v):
            scale = g * lax.rsqrt(v + EPS)
            return (x - m[:, None, None]) * scale[:, None, None] + b[:, None, None]

        def _cond_conv(x, experts, rw, stride, padding):
            W = jnp.einsum('be,eoihw->boihw', rw, experts)

            def one(xi, wi):
                return lax.conv_general_dilated(xi[None], wi, (stride, stride), [(padding, padding)] * 2, dimension_numbers=('NCHW', 'OIHW', 'NCHW'))[0]
            return jax.vmap(one)(x, W)

        def _forward(x, router_w, router_b, w1, w2, w3, g1, b1, m1, v1, g2, b2, m2, v2, g3, b3, m3, v3):
            pooled = x.mean(axis=(2, 3))
            rw = jax.nn.sigmoid(pooled @ router_w.T + router_b)
            out = _cond_conv(x, w1, rw, 1, 0)
            out = jax.nn.relu(_bn(out, g1, b1, m1, v1))
            out = _cond_conv(out, w2, rw, 1, 1)
            out = jax.nn.relu(_bn(out, g2, b2, m2, v2))
            out = _cond_conv(out, w3, rw, 1, 0)
            out = _bn(out, g3, b3, m3, v3)
            return jax.nn.relu(out + x)
        key = jax.random.key(seed)
        ks = jax.random.split(key, 8)
        B, Cin, H, W = (32, 256, 28, 28)
        E, width, Cout = (8, 64, 256)

        def rnd(k, shape, scale=0.05):
            return jax.random.normal(k, shape, dtype=jnp.float32) * scale
        return {'x': jax.random.normal(ks[0], (B, Cin, H, W), dtype=jnp.float32), 'router_w': rnd(ks[1], (E, Cin)), 'router_b': jnp.zeros((E,), jnp.float32), 'w1': rnd(ks[2], (E, width, Cin, 1, 1)), 'w2': rnd(ks[3], (E, width, width, 3, 3)), 'w3': rnd(ks[4], (E, Cout, width, 1, 1)), 'g1': jnp.ones((width,), jnp.float32), 'b1': jnp.zeros((width,), jnp.float32), 'm1': jnp.zeros((width,), jnp.float32), 'v1': jnp.ones((width,), jnp.float32), 'g2': jnp.ones((width,), jnp.float32), 'b2': jnp.zeros((width,), jnp.float32), 'm2': jnp.zeros((width,), jnp.float32), 'v2': jnp.ones((width,), jnp.float32), 'g3': jnp.ones((Cout,), jnp.float32), 'b3': jnp.zeros((Cout,), jnp.float32), 'm3': jnp.zeros((Cout,), jnp.float32), 'v3': jnp.ones((Cout,), jnp.float32)}
    _L1_conv_all = _L1_conv_setup()
    _L1_conv_in = {k: v for k, v in _L1_conv_all.items() if k in ('router_w', 'router_b', 'w1', 'w2', 'w3', 'g1', 'b1', 'm1', 'v1', 'g2', 'b2', 'm2', 'v2', 'g3', 'b3', 'm3', 'v3')}
    del _L1_conv_all
    return {'x': x, 'L0_conv_gn_w': _L0_conv_in['gn_w'], 'L0_conv_gn_b': _L0_conv_in['gn_b'], 'L0_conv_qkv_w': _L0_conv_in['qkv_w'], 'L0_conv_qkv_b': _L0_conv_in['qkv_b'], 'L0_conv_proj_w': _L0_conv_in['proj_w'], 'L0_conv_proj_b': _L0_conv_in['proj_b'], 'L1_conv_router_w': _L1_conv_in['router_w'], 'L1_conv_router_b': _L1_conv_in['router_b'], 'L1_conv_w1': _L1_conv_in['w1'], 'L1_conv_w2': _L1_conv_in['w2'], 'L1_conv_w3': _L1_conv_in['w3'], 'L1_conv_g1': _L1_conv_in['g1'], 'L1_conv_b1': _L1_conv_in['b1'], 'L1_conv_m1': _L1_conv_in['m1'], 'L1_conv_v1': _L1_conv_in['v1'], 'L1_conv_g2': _L1_conv_in['g2'], 'L1_conv_b2': _L1_conv_in['b2'], 'L1_conv_m2': _L1_conv_in['m2'], 'L1_conv_v2': _L1_conv_in['v2'], 'L1_conv_g3': _L1_conv_in['g3'], 'L1_conv_b3': _L1_conv_in['b3'], 'L1_conv_m3': _L1_conv_in['m3'], 'L1_conv_v3': _L1_conv_in['v3']}

def reference(x, L0_conv_gn_w, L0_conv_gn_b, L0_conv_qkv_w, L0_conv_qkv_b, L0_conv_proj_w, L0_conv_proj_b, L1_conv_router_w, L1_conv_router_b, L1_conv_w1, L1_conv_w2, L1_conv_w3, L1_conv_g1, L1_conv_b1, L1_conv_m1, L1_conv_v1, L1_conv_g2, L1_conv_b2, L1_conv_m2, L1_conv_v2, L1_conv_g3, L1_conv_b3, L1_conv_m3, L1_conv_v3):
    import jax
    import jax.numpy as jnp

    def _L0_conv_ref(x, gn_w, gn_b, qkv_w, qkv_b, proj_w, proj_b):
        import math
        import jax, jax.numpy as jnp
        import numpy as np
        CH = 256
        NUM_HEADS = 4
        GROUPS = 32
        EPS = 1e-05

        def group_norm(x, gamma, beta):
            b, c, h, w = x.shape
            xg = x.reshape(b, GROUPS, c // GROUPS, h * w)
            mean = jnp.mean(xg, axis=(2, 3), keepdims=True)
            var = jnp.var(xg, axis=(2, 3), keepdims=True)
            xn = (xg - mean) * jax.lax.rsqrt(var + EPS)
            xn = xn.reshape(b, c, h, w)
            return xn * gamma[None, :, None, None] + beta[None, :, None, None]
        b, c, h, w = x.shape
        head_dim = c // NUM_HEADS
        xn = group_norm(x, gn_w, gn_b)
        qkv = jnp.einsum('oc,bchw->bohw', qkv_w, xn) + qkv_b[None, :, None, None]
        q, k, v = jnp.split(qkv, 3, axis=1)
        n = h * w
        q = q.reshape(b, NUM_HEADS, head_dim, n)
        k = k.reshape(b, NUM_HEADS, head_dim, n)
        v = v.reshape(b, NUM_HEADS, head_dim, n)
        attn = jnp.einsum('bhdm,bhdn->bhmn', q, k) / math.sqrt(head_dim)
        attn = jax.nn.softmax(attn, axis=-1)
        out = jnp.einsum('bhmn,bhdn->bhdm', attn, v).reshape(b, c, h, w)
        out = jnp.einsum('oc,bchw->bohw', proj_w, out) + proj_b[None, :, None, None]
        return x + out

    def _L1_conv_ref(x, router_w, router_b, w1, w2, w3, g1, b1, m1, v1, g2, b2, m2, v2, g3, b3, m3, v3):
        import jax, jax.numpy as jnp
        import numpy as np
        from jax import lax
        EPS = 1e-05

        def _bn(x, g, b, m, v):
            scale = g * lax.rsqrt(v + EPS)
            return (x - m[:, None, None]) * scale[:, None, None] + b[:, None, None]

        def _cond_conv(x, experts, rw, stride, padding):
            W = jnp.einsum('be,eoihw->boihw', rw, experts)

            def one(xi, wi):
                return lax.conv_general_dilated(xi[None], wi, (stride, stride), [(padding, padding)] * 2, dimension_numbers=('NCHW', 'OIHW', 'NCHW'))[0]
            return jax.vmap(one)(x, W)

        def _forward(x, router_w, router_b, w1, w2, w3, g1, b1, m1, v1, g2, b2, m2, v2, g3, b3, m3, v3):
            pooled = x.mean(axis=(2, 3))
            rw = jax.nn.sigmoid(pooled @ router_w.T + router_b)
            out = _cond_conv(x, w1, rw, 1, 0)
            out = jax.nn.relu(_bn(out, g1, b1, m1, v1))
            out = _cond_conv(out, w2, rw, 1, 1)
            out = jax.nn.relu(_bn(out, g2, b2, m2, v2))
            out = _cond_conv(out, w3, rw, 1, 0)
            out = _bn(out, g3, b3, m3, v3)
            return jax.nn.relu(out + x)
        return _forward(x, router_w, router_b, w1, w2, w3, g1, b1, m1, v1, g2, b2, m2, v2, g3, b3, m3, v3)

    def _gn(v, G=32, eps=1e-05):
        B_, C_, H_, W_ = v.shape
        g = v.reshape(B_, G, C_ // G, H_, W_)
        m = jnp.mean(g, axis=(2, 3, 4), keepdims=True)
        s = jnp.var(g, axis=(2, 3, 4), keepdims=True)
        return ((g - m) / jnp.sqrt(s + eps)).reshape(v.shape)

    def _ln_c(v, eps=1e-06):
        m = jnp.mean(v, axis=1, keepdims=True)
        s = jnp.var(v, axis=1, keepdims=True)
        return (v - m) / jnp.sqrt(s + eps)

    def _ln_t(v, eps=1e-05):
        m = jnp.mean(v, axis=-1, keepdims=True)
        s = jnp.var(v, axis=-1, keepdims=True)
        return (v - m) / jnp.sqrt(s + eps)

    def _to_tokens(v):
        B_, C_, H_, W_ = v.shape
        return v.reshape(B_, C_, H_ * W_).transpose(0, 2, 1)

    def _from_tokens(t, like):
        B_, C_, H_, W_ = like.shape
        return t.transpose(0, 2, 1).reshape(B_, C_, H_, W_)
    x = _L0_conv_ref(x, L0_conv_gn_w, L0_conv_gn_b, L0_conv_qkv_w, L0_conv_qkv_b, L0_conv_proj_w, L0_conv_proj_b)
    x = _L1_conv_ref(x, L1_conv_router_w, L1_conv_router_b, L1_conv_w1, L1_conv_w2, L1_conv_w3, L1_conv_g1, L1_conv_b1, L1_conv_m1, L1_conv_v1, L1_conv_g2, L1_conv_b2, L1_conv_m2, L1_conv_v2, L1_conv_g3, L1_conv_b3, L1_conv_m3, L1_conv_v3)
    return x

_drawn_inputs = setup_inputs


def setup_inputs(seed=0):
    import zlib

    import numpy as np

    out = dict(_drawn_inputs(seed))
    spreads = {'L0_conv_gn_w': (1.0, 0.2),
     'L0_conv_gn_b': (0.0, 0.1),
     'L0_conv_qkv_b': (0.0, 0.1),
     'L0_conv_proj_b': (0.0, 0.1),
     'L1_conv_router_b': (0.0, 0.1),
     'L1_conv_g1': (1.0, 0.2),
     'L1_conv_b1': (0.0, 0.1),
     'L1_conv_m1': (0.0, 0.1),
     'L1_conv_v1': (1.0, 0.2),
     'L1_conv_g2': (1.0, 0.2),
     'L1_conv_b2': (0.0, 0.1),
     'L1_conv_m2': (0.0, 0.1),
     'L1_conv_v2': (1.0, 0.2),
     'L1_conv_g3': (1.0, 0.2),
     'L1_conv_b3': (0.0, 0.1),
     'L1_conv_m3': (0.0, 0.1),
     'L1_conv_v3': (1.0, 0.2)}
    factors = {}
    for name, (base, spread) in spreads.items():
        noise = np.random.default_rng([zlib.crc32(name.encode()), seed]).standard_normal(out[name].shape)
        drawn = base * np.exp(spread * noise) if base else spread * noise
        out[name] = jnp.asarray(drawn.astype(out[name].dtype))
    for name, factor in factors.items():
        out[name] = (out[name] * factor).astype(out[name].dtype)
    return out
```

```python
from contextlib import ExitStack

import numpy as np

import concourse.bass as bass
from concourse import mybir

F32 = mybir.dt.float32
F32R = mybir.dt.float32r
ALU = mybir.AluOpType
ACT = mybir.ActivationFunctionType
AX = mybir.AxisListType

B, C, H, W = 16, 256, 32, 32
N = H * W
P = 128
CC = C // P
HEADS, D = 4, 64
PAIRS = HEADS // 2
HALF = 512
NH = N // HALF
KT = N // P
QT = HALF // P
BLOCKS = PAIRS * NH
STEPS = BLOCKS * KT
GROUP = 8
SUBSETS = 2 * NH
E = 8
WID = 64
EPS = 1e-5
PW = W + 2
PAD = (H + 2) * PW
TAPS = 6
M1, M2, M3 = CC * WID, TAPS * WID, C
MIX = M1 + M2 + M3
PBUF = 4

V_GNW, V_GNB, V_QKVB, V_PROJB, V_G, V_B, V_M, V_V = 0, 2, 4, 10, 12, 16, 20, 24
VECS = 28

SIDE = {
    0: [("qk", 0, 4)], 1: [("qk", 0, 5)], 2: [("z", -1, 3)], 3: [("qk", 0, 6)], 4: [("qk", 0, 7)],
    5: [("proj", -1, 0)], 6: [("proj", -1, 1)], 7: [("proj", -1, 2)], 8: [("proj", -1, 3)],
    9: [("gna", 1, 0)], 10: [("gnb", 1, 0)], 11: [("z", 0, 0)], 12: [("router", -1, 0)],
    16: [("qk", 1, 0)], 17: [("qk", 1, 1)], 18: [("z", 0, 1)], 19: [("qk", 1, 2)], 20: [("qk", 1, 3)],
    21: [("conv1", -1, 0)], 23: [("conv2a", -1, 0)], 24: [("conv2", -1, 0)], 25: [("v", 1, 0)],
    26: [("z", 0, 2)], 27: [("v", 1, 1)], 28: [("v", 1, 2), ("conv3", -1, 0)],
    29: [("v", 1, 3), ("conv3", -1, 1)], 30: [("conv3", -1, 2)], 31: [("conv3", -1, 3)],
}
PROLOGUE = [("gna", 0, 0), ("gnb", 0, 0)] + [("qk", 0, f) for f in range(4)] + [("v", 0, f) for f in range(4)]
EPILOGUE = ([("z", 0, 3)] + [("proj", 0, f) for f in range(4)] + [("router", 0, 0), ("conv1", 0, 0),
            ("conv2a", 0, 0), ("conv2", 0, 0)] + [("conv3", 0, f) for f in range(4)])
MAXFILLS = {0: (1, range(4, 6)), 1: (1, range(6, 8)), 2: (1, range(8, 10)), 3: (1, range(10, 13)), 4: (1, range(13, 16)),
            6: (2, range(0, 2)), 7: (2, range(2, 4))}
ROWSTEP = 5
STATS_STEPS, AFFINE_STEP, NORM_STEP, SPLIT_STEPS = (7, 8), 11, 12, (13, 14)
MIX_STEPS = {13: 1, 14: 1, 15: 2, 16: 1, 17: 1, 18: 1, 19: 1}


def build(nc, x, vecs, router_b, wqkv, wproj, wrouter, experts, neg_eye, group_avg, out):
    ctx = ExitStack()
    with ctx:
        def sb(name, shape, dt=F32):
            return ctx.enter_context(nc.sbuf_tensor(name, shape, dt))

        def pb(name, shape):
            return ctx.enter_context(nc.psum_tensor(name, shape, F32))

        def sem(name):
            return ctx.enter_context(nc.semaphore(name))

        vec = sb("vec", [P, VECS])
        rbias = sb("rbias", [P, E])
        w_hi = sb("w_hi", [P, CC, 3 * C], F32R)
        w_lo = sb("w_lo", [P, CC, 3 * C], F32R)
        wp = sb("wp", [P, CC, C])
        wr = sb("wr", [P, CC, E])
        ex = sb("ex", [P, E, MIX])
        negeye = sb("negeye", [P, P])
        gavg = sb("gavg", [P, P])
        ones = sb("ones", [P, P])
        neghalf = sb("neghalf", [P, 4])
        pbias = sb("pbias", [P, CC])
        bn_var = sb("bn_var", [P, 4])
        bn_rs = sb("bn_rs", [P, 4])
        bn_s = sb("bn_s", [P, 4])
        bn_ms = sb("bn_ms", [P, 4])
        bn_c = sb("bn_c", [P, 4])
        xin = sb("xin", [P, CC, N])
        x_hi = sb("x_hi", [P, CC, N], F32R)
        x_lo = sb("x_lo", [P, CC, N], F32R)
        Q1 = sb("Q1", [P, HEADS, N], F32R)
        Q2 = sb("Q2", [P, HEADS, N], F32R)
        K1 = sb("K1", [P, HEADS, N], F32R)
        K2 = sb("K2", [P, HEADS, N], F32R)
        V = sb("V", [P, PAIRS, KT, P])
        v_next = sb("v_next", [P, KT, P])
        prob = sb("prob", [P, PBUF, 2, HALF])
        w_stage = prob[:, :, :, :].rearrange("p b a n -> p (b a n)")[:, 0:CC * 3 * C].rearrange("p (c n) -> p c n", c=CC)
        psum_p = sb("psum_p", [P, 2, 2, HALF])
        o_raw = sb("o_raw", [P, 2, HALF])
        rz = sb("rz", [P, 2, HALF])
        o = sb("o", [P, CC, N])
        x2 = sb("x2", [P, CC, N])
        hpad = sb("hpad", [P, PAD + 2])
        h2 = sb("h2", [P, HALF])
        y = sb("y", [P, 2, HALF])
        mix = sb("mix", [P, MIX])
        mix3 = sb("mix3", [P, NH, C])
        mx = sb("mx", [P, 2 * QT, NH])
        mx1 = sb("mx1", [P, 2 * QT])
        mrow = sb("mrow", [2 * QT, P], F32R)
        bst = sb("bst", [P, CC, SUBSETS, 3])
        gsum = sb("gsum", [P, CC, 3])
        gdev = sb("gdev", [P, CC, SUBSETS])
        gdev2 = sb("gdev2", [P, CC, SUBSETS])
        gvar_in = sb("gvar_in", [P, CC])
        gvar_of = sb("gvar_of", [P, CC])
        gvar = sb("gvar", [P, CC])
        grs = sb("grs", [P, CC])
        gsc = sb("gsc", [P, CC])
        gms = sb("gms", [P, CC])
        gbi = sb("gbi", [P, CC])
        pool4 = sb("pool4", [P, CC, NH])
        pool2 = sb("pool2", [P, CC])
        poolb = sb("poolb", [P, CC, P])
        logit = sb("logit", [P, E])
        rexp = sb("rexp", [P, E])
        rden = sb("rden", [P, E])
        rw = sb("rw", [P, E])

        S = pb("S", [P, 2, 2, HALF])
        MS = pb("MS", [P, 2, HALF])
        PV = pb("PV", [P, HALF])
        SB = pb("SB", [P, HALF])

        const_loaded = sem("const_loaded")
        consts_set = sem("consts_set")
        dve_set = sem("dve_set")
        bias_filled = sem("bias_filled")
        bn_pow = sem("bn_pow")
        xin_loaded = sem("xin_loaded")
        x2_loaded = sem("x2_loaded")
        v1_loaded = sem("v1_loaded")
        rows_loaded = sem("rows_loaded")
        dup_loaded = sem("dup_loaded")
        y_stored = [sem(f"y{n}_stored") for n in range(2)]
        s_done = sem("s_done")
        exp_done = sem("exp_done")
        pv_done = sem("pv_done")
        add_done = sem("add_done")
        o_saved = sem("o_saved")
        o_norm = sem("o_norm")
        rz_ready = sem("rz_ready")
        max_filled = sem("max_filled")
        max_read = sem("max_read")
        max_ready = sem("max_ready")
        row_filled = sem("row_filled")
        row_read = sem("row_read")
        filled = {k: sem(k + "_filled") for k in ("qk", "v", "z", "proj", "gna", "gnb", "router", "conv1", "conv2", "conv3")}
        read = {k: sem(k + "_read") for k in ("qk", "v", "z", "proj", "gna", "gnb", "router", "conv1", "conv2", "conv3")}
        per_image = {"qk": 8, "v": 4, "z": 4, "proj": 4, "gna": 1, "gnb": 1, "router": 1, "conv1": 1, "conv2": 1, "conv3": 4}
        qk_hi = sem("qk_hi")
        stats_ready = sem("stats_ready")
        gvar_part = sem("gvar_part")
        gvar_ready = sem("gvar_ready")
        dev_done = sem("dev_done")
        dev2_ready = sem("dev2_ready")
        rs_ready = sem("rs_ready")
        aff = sem("aff")
        xn_ready = sem("xn_ready")
        xhi_ready = sem("xhi_ready")
        xsplit_ready = sem("xsplit_ready")
        pool_done = sem("pool_done")
        rexp_ready = sem("rexp_ready")
        rw_chain = sem("rw_chain")
        mix_chain = sem("mix_chain")
        mix_ready = sem("mix_ready")
        y_ready = sem("y_ready")

        LOADS, DVE_SET, CONSTS_SET = 8, 7, 4 + 3 * HEADS

        block = ctx.enter_context(nc.Block())

        def wait(eng, s, value):
            if not isinstance(value, int) or value > 0:
                eng.wait_ge(s, value)

        def adds_reading(g_image, s):
            return g_image * (STEPS - BLOCKS) + (s // KT) * (KT - 1) + max(1, s % KT)

        def done(kind, i, f):
            return per_image[kind] * i + f + 1

        def jobs_of(s, first, last):
            gone = {-1} if first else set()
            gone |= {1} if last else set()
            return [j for j in SIDE.get(s, []) if j[1] not in gone]

        def sections(eng, section):
            section(0, True, False)
            section(1, False, False)
            with eng.Fori(2, B - 1) as i:
                section(i, False, False)
            section(B - 1, False, True)

        def fills_at(i, s, last):
            ahead, fills = MAXFILLS.get(s % KT, (0, ()))
            b = s // KT + ahead
            return [] if last and b >= BLOCKS else [(i + b // BLOCKS, b % BLOCKS, m) for m in fills]

        PROLOGUE_FILLS = [(0, 0, m) for m in range(16)] + [(0, 1, m) for m in range(MAXFILLS[0][1][0])]

        def own(a):
            return slice(64 * a, 64 * a + 64)

        def other(a):
            return slice(64 - 64 * a, 128 - 64 * a)

        def px(hf):
            return slice(hf * HALF, hf * HALF + HALF)

        @block.sync
        def _(sp):
            def load_xin(i):
                if not isinstance(i, int) or i > 0:
                    wait(sp, xsplit_ready, 2 * i)
                sp.dma_start(xin[:, :, :], x[i]).then_inc(xin_loaded, 16)

            def load_x2(i):
                wait(sp, read["conv3"], 4 * i)
                sp.dma_start(x2[:, :, :], x[i]).then_inc(x2_loaded, 16)

            def load_v1(i):
                sp.wait_ge(pv_done, STEPS * i + 1)
                sp.dma_start(V[:, 1, :, :], v_next[:, :, :]).then_inc(v1_loaded, 16)

            def dup(i, f):
                p, kind, hf = f // 4, f % 4 // 2, f % 2
                sp.wait_ge(qk_hi, 8 * i + f + 1)
                for a in range(2):
                    h = 2 * p + a
                    if kind:
                        src, dst = Q1[own(a), h, px(hf)], Q1[other(a), h, px(hf)]
                    else:
                        src, dst = K1[own(a), h, px(hf)], K2[own(a), h, px(hf)]
                    sp.dma_start(dst.bitcast(F32), src.bitcast(F32)).then_inc(dup_loaded, 16)

            def rows(i, b):
                p, hf = b // NH, b % NH
                sp.wait_ge(row_read, BLOCKS * i + b + 1)
                for a in range(2):
                    r = 64 - 64 * a
                    sp.dma_start(Q2[r:r + 1, 2 * p + a, px(hf)].bitcast(F32),
                                 mrow[QT * a:QT * a + QT, :].bitcast(F32)).then_inc(rows_loaded, 16)

            def store(i, f):
                oc, hf = f // NH, f % NH
                wait(sp, y_ready, 4 * i + f + 1)
                sp.dma_start(out[i, :, oc, px(hf)], y[:, f % 2, :]).then_inc(y_stored[f % 2], 16)

            def section(i, first, last):
                load_v1(i)
                for s in range(STEPS):
                    for kind, di, f in jobs_of(s, first, last):
                        if kind == "qk":
                            dup(i + di, f)
                    if s == 1 and not first:
                        load_x2(i - 1)
                    if s % KT == ROWSTEP and not (last and s > STEPS - KT):
                        b = s // KT + 1
                        rows(i + b // BLOCKS, b % BLOCKS)
                    if s == 0 and not last:
                        load_xin(i + 1)
                    if not first and s >= 29:
                        store(i - 1, s - 29)
                if not first:
                    store(i - 1, 3)

            sp.dma_start(vec[:, :], vecs).then_inc(const_loaded, 16)
            load_xin(0)
            sp.dma_start(w_stage, wqkv).then_inc(const_loaded, 16)
            sp.dma_start(gavg[:, :], group_avg).then_inc(const_loaded, 16)
            sp.dma_start(negeye[:, :], neg_eye).then_inc(const_loaded, 16)
            sp.dma_start(wp[:, :, :], wproj).then_inc(const_loaded, 16)
            sp.dma_start(wr[:, :, :], wrouter).then_inc(const_loaded, 16)
            sp.dma_start(rbias[:, :], router_b).then_inc(const_loaded, 16)
            sp.dma_start(ex[:, :, :], experts).then_inc(const_loaded, 16)
            for f in range(4):
                dup(0, f)
            rows(0, 0)
            sections(sp, section)
            load_x2(B - 1)
            for f in range(4):
                store(B - 1, f)
            for n in range(2):
                sp.wait_ge(y_stored[n], 16 * 2 * B)

        @block.gpsimd
        def _(pool):
            count = 0
            fills = [(neghalf[:, :], -0.5), (ones[:, :], 1.0), (hpad[:, :], 0.0), (mix3[:, :, :], 0.0)]
            for h in range(HEADS):
                r = 64 - 64 * (h % 2)
                fills += [(t[other(h % 2), h, :].bitcast(F32), 0.0) for t in (Q2, K2)]
                fills += [(K2[r:r + 1, h, :].bitcast(F32), 1.0)]
            for dst, value in fills:
                nc.gpsimd.memset(dst, value).then_inc(consts_set, 1)
                count += 1
                pool.wait_ge(consts_set, count)
            pool.wait_ge(dve_set, 1)
            nc.gpsimd.tensor_tensor(bn_rs[:, :], bn_var[:, :], neghalf[:, :], ALU.pow).then_inc(bn_pow, 1)

            def rstd(i):
                pool.wait_ge(gvar_ready, i + 1)
                nc.gpsimd.tensor_tensor(grs[:, :], gvar[:, :], neghalf[:, 0:CC], ALU.pow).then_inc(rs_ready, 1)

            def section(i, first, last):
                for s in range(STEPS):
                    b, j = s // KT, s % KT
                    acc = psum_p[:, b % 2, :, :]
                    if j == 1:
                        wait(pool, filled["z"], BLOCKS * i + b - 1)
                    if j > 0:
                        pool.wait_ge(exp_done, STEPS * i + s + 1)
                        if j > 1:
                            pool.wait_ge(add_done, adds_reading(i, s) - 1)
                        first_in = prob[:, (s - 1) % PBUF, :, :] if j == 1 else acc
                        nc.gpsimd.tensor_tensor(acc, first_in, prob[:, s % PBUF, :, :], ALU.add).then_inc(add_done, 1)
                    if s == 11 and not last:
                        rstd(i + 1)

            rstd(0)
            sections(pool, section)

        @block.tensor
        def _(pe):
            def split_mm(dst, wl, xl, pairs):
                k = 0
                for c in range(CC):
                    for w, m in pairs:
                        last = nc.tensor.matmul(dst, wl(w, c), xl(m, c), start=(k == 0), stop=(k == 3 * CC - 1))
                        k += 1
                return last

            def job(kind, i, f, before):
                for k, bi, bf in before:
                    pe.wait_ge(read[k], done(k, bi, bf))
                if kind == "gna":
                    pe.wait_ge(stats_ready, CC * i + CC)
                    last = nc.tensor.matmul(SB[:, 0:CC * SUBSETS * 3], gavg[:, :], bst[:, :, :, :].rearrange("p c s k -> p (c s k)"), start=True, stop=True)
                elif kind == "gnb":
                    pe.wait_ge(dev2_ready, i + 1)
                    last = nc.tensor.matmul(SB[:, 0:CC * SUBSETS], gavg[:, :], gdev2[:, :, :].rearrange("p c s -> p (c s)"), start=True, stop=True)
                elif kind == "qk":
                    p, isq, hf = f // 4, f % 4 // 2, f % 2
                    if f == 0:
                        pe.wait_ge(xsplit_ready, 2 * i + 2)
                    col = (0 if isq else C) + p * P
                    last = split_mm(SB[:, :], lambda w, c: w[:, c, col:col + P], lambda m, c: m[:, c, px(hf)],
                                    ((w_hi, x_hi), (w_hi, x_lo), (w_lo, x_hi)))
                elif kind == "v":
                    for t in (0, 1):
                        kt = 2 * f + t
                        last = split_mm(SB[:, t * C:t * C + C], lambda w, c: w[:, c, kt * P:kt * P + P],
                                        lambda m, c: m[:, c, 2 * C:3 * C], ((x_hi, w_hi), (x_lo, w_hi), (x_hi, w_lo)))
                elif kind == "z":
                    pe.wait_ge(add_done, adds_reading(i, KT * f + KT - 1))
                    for a in range(2):
                        last = nc.tensor.matmul(SB[own(a), :], ones[:, 0:D], psum_p[:, f % 2, a, :], start=True, stop=True)
                elif kind == "proj":
                    oc, hf = f // NH, f % NH
                    if f == 0:
                        pe.wait_ge(o_norm, BLOCKS * i + BLOCKS)
                    for c in range(CC):
                        last = nc.tensor.matmul(SB[:, :], wp[:, c, oc * P:oc * P + P], o[:, c, px(hf)],
                                                start=(c == 0), stop=(c == CC - 1))
                elif kind == "router":
                    pe.wait_ge(pool_done, 2 * i + 2)
                    for c in range(CC):
                        last = nc.tensor.matmul(SB[:, 0:E], poolb[:, c, :], wr[:, c, :], start=(c == 0), stop=(c == CC - 1))
                elif kind == "conv1":
                    pe.wait_ge(mix_ready, i + 1)
                    for c in range(CC):
                        for hf in range(NH):
                            last = nc.tensor.matmul(SB[own(hf), :], mix[:, c * WID:c * WID + WID], x2[:, c, px(hf)],
                                                    start=(c == 0), stop=(c == CC - 1))
                elif kind in ("conv2a", "conv2"):
                    rows_hf = H // NH
                    for tap in (range(3) if kind == "conv2a" else range(3, 6)):
                        dy, dx = tap % 3, 2 * (tap // 3)
                        for hf in range(NH):
                            at = (dy + hf * rows_hf) * PW + dx
                            src = hpad[:, at:at + rows_hf * PW].rearrange("p (r w) -> p r w", w=PW)[:, :, 0:W]
                            last = nc.tensor.matmul(SB[own(hf), :], mix[:, M1 + tap * WID:M1 + tap * WID + WID], src,
                                                    start=(tap == 0), stop=(tap == TAPS - 1))
                elif kind == "conv3":
                    oc, hf = f // NH, f % NH
                    if f == 0:
                        pe.wait_ge(read["conv2"], i + 1)
                    last = nc.tensor.matmul(SB[:, :], mix3[:, hf, oc * P:oc * P + P], h2[:, :], start=True, stop=True)
                if kind != "conv2a":
                    last.then_inc(filled[kind], 1)

            def max_fill(i, b, m):
                p, hf, a, t, nh = b // NH, b % NH, m // (2 * QT), m // 2 % QT, m % 2
                h = 2 * p + a
                if m == 0:
                    pe.wait_ge(read["qk"], 8 * i + 4 * p + 4)
                    pe.wait_ge(dup_loaded, 32 * (8 * i + 4 * p + 4))
                    wait(pe, row_read, BLOCKS * i + b)
                wait(pe, max_read, 64 * i + 16 * b + m - 1)
                q0 = hf * HALF + t * P
                nc.tensor.matmul(MS[:, m % 2, :], Q1[:, h, q0:q0 + P], K1[:, h, px(nh)],
                                 start=True, stop=True).then_inc(max_filled, 1)

            def max_row(i, b):
                pe.wait_ge(max_ready, BLOCKS * i + b + 1)
                nc.tensor.matmul(MS[0:2 * QT, 0, 0:P], mx1[:, :], negeye[:, :], start=True, stop=True).then_inc(row_filled, 1)

            def scores(i, s):
                b, kt = s // KT, s % KT
                p, hf = b // NH, b % NH
                wait(pe, exp_done, STEPS * i + s - 1)
                for a in range(2):
                    h = 2 * p + a
                    nc.tensor.matmul(S[:, s % 2, a, :], K1[:, h, kt * P:kt * P + P], Q1[:, h, px(hf)], start=True, stop=False)
                    if kt == 0 and a == 0:
                        pe.wait_ge(rows_loaded, 32 * (BLOCKS * i + b + 1))
                    last = nc.tensor.matmul(S[:, s % 2, a, :], K2[:, h, kt * P:kt * P + P], Q2[:, h, px(hf)], start=False, stop=True)
                last.then_inc(s_done, 1)

            def pv(i, s):
                b, kt = s // KT, s % KT
                if s == 0:
                    pe.wait_ge(read["v"], 4 * i + 4)
                if s == KT * NH:
                    pe.wait_ge(v1_loaded, 16 * i + 16)
                if kt == 0:
                    wait(pe, o_saved, BLOCKS * i + b)
                pe.wait_ge(exp_done, STEPS * i + s + 1)
                for a in range(2):
                    last = nc.tensor.matmul(PV[own(a), :], V[:, b // NH, kt, a * D:a * D + D], prob[:, s % PBUF, a, :],
                                            start=(kt == 0), stop=(kt == KT - 1))
                last.then_inc(pv_done, 1)

            pe.wait_ge(const_loaded, 16 * LOADS)
            for oc in range(CC):
                for c in range(CC):
                    last = nc.tensor.matmul(MS[:, 0, oc:oc + 1], wp[:, c, oc * P:oc * P + P], vec[:, V_QKVB + 4 + c:V_QKVB + 5 + c],
                                            start=(c == 0), stop=(c == CC - 1))
            last.then_inc(bias_filled, 1)
            pe.wait_ge(consts_set, CONSTS_SET)
            before = []
            for kind, i, f in PROLOGUE:
                job(kind, i, f, before)
                before = [(kind, i, f)]
            pe.wait_ge(dve_set, DVE_SET)
            for at in PROLOGUE_FILLS[:16]:
                max_fill(*at)
            max_row(0, 0)
            for at in PROLOGUE_FILLS[16:]:
                max_fill(*at)
            scores(0, 0)

            def section(i, first, last):
                held = [("v", i, 3)] + ([] if first else [("conv3", i - 2, 3)])
                for s in range(STEPS):
                    fills = fills_at(i, s, last)
                    jobs = jobs_of(s, first, last)
                    if s < STEPS - 1:
                        scores(i, s + 1)
                    elif not last:
                        scores(i + 1, 0)
                    for at in fills[0:1]:
                        max_fill(*at)
                    if s % KT == ROWSTEP and not (last and s > STEPS - KT):
                        b = s // KT + 1
                        max_row(i + b // BLOCKS, b % BLOCKS)
                    for kind, di, f in jobs[0:1]:
                        job(kind, i + di, f, [] if kind == "conv2" else held)
                        held = [(kind, i + di, f)]
                    for at in fills[1:2]:
                        max_fill(*at)
                    pv(i, s)
                    for at in fills[2:]:
                        max_fill(*at)
                    for kind, di, f in jobs[1:]:
                        job(kind, i + di, f, held)
                        held = [(kind, i + di, f)]

            sections(pe, section)
            held = [("conv3", B - 2, 3)]
            for kind, _, f in EPILOGUE:
                job(kind, B - 1, f, [] if kind == "conv2" else held)
                held = [(kind, B - 1, f)]

        @block.scalar
        def _(act):
            def exps(i, s):
                wait(act, pv_done, STEPS * i + s - PBUF + 1)
                wait(act, add_done, adds_reading(i, s - PBUF) if s >= PBUF else
                     (adds_reading(i - 1, STEPS + s - PBUF) if not isinstance(i, int) or i > 0 else 0))
                act.wait_ge(s_done, STEPS * i + s + 1)
                nc.scalar.activation(prob[:, s % PBUF, :, :], S[:, s % 2, :, :], ACT.Exp, scale=D ** -0.5).then_inc(exp_done, 1)

            def save_o(i, b):
                act.wait_ge(pv_done, STEPS * i + KT * b + KT)
                wait(act, o_norm, BLOCKS * i + b - 1)
                nc.scalar.activation(o_raw[:, b % 2, :], PV[:, :], ACT.Copy).then_inc(o_saved, 1)

            def job(kind, i, f):
                if kind == "qk":
                    p, isq, hf = f // 4, f % 4 // 2, f % 2
                    act.wait_ge(filled["qk"], 8 * i + f + 1)
                    wait(act, s_done, STEPS * (i - 1) + KT * NH * (p + 1))
                    dst = Q1 if isq else K1
                    col = V_QKVB + (0 if isq else 2) + p
                    for a in range(2):
                        last = nc.scalar.activation(dst[own(a), 2 * p + a, px(hf)], SB[own(a), :], ACT.Identity,
                                                    bias=vec[own(a), col:col + 1])
                    last.then_inc(qk_hi, 1)
                elif kind == "v":
                    act.wait_ge(filled["v"], 4 * i + f + 1)
                    wait(act, pv_done, STEPS * (i - 1) + KT * NH)
                    wait(act, v1_loaded, 16 * i)
                    src = SB[:, :].rearrange("p (t q n) -> p t q n", t=2, q=PAIRS)
                    nc.scalar.activation(V[:, 0, 2 * f:2 * f + 2, :], src[:, :, 0, :], ACT.Copy)
                    nc.scalar.activation(v_next[:, 2 * f:2 * f + 2, :], src[:, :, 1, :], ACT.Copy).then_inc(read["v"], 1)
                elif kind == "z":
                    act.wait_ge(filled["z"], 4 * i + f + 1)
                    wait(act, o_norm, 4 * i + f - 1)
                    nc.scalar.activation(rz[:, f % 2, :], SB[:, :], ACT.Copy).then_inc(read["z"], 1)
                elif kind == "router":
                    act.wait_ge(read["router"], i + 1)
                    nc.scalar.activation(rexp[:, :], logit[:, :], ACT.Exp, scale=-1.0).then_inc(rexp_ready, 1)
                elif kind == "conv1":
                    act.wait_ge(filled["conv1"], i + 1)
                    rows_hf = H // NH
                    for hf in range(NH):
                        for copy in range(2):
                            at = (1 + hf * rows_hf) * PW + 1 - copy
                            dst = hpad[own(copy), at:at + rows_hf * PW].rearrange("p (r w) -> p r w", w=PW)[:, :, 0:W]
                            src = SB[own(hf), :].rearrange("p (r w) -> p r w", w=W)
                            last = nc.scalar.activation(dst, src, ACT.Relu, bias=bn_c[own(hf), 0:1], scale=bn_s[own(hf), 0:1])
                    last.then_inc(read["conv1"], 1)
                elif kind == "conv2":
                    act.wait_ge(filled["conv2"], i + 1)
                    nc.scalar.activation(h2[:, :], SB[:, :], ACT.Relu, bias=bn_c[:, 1:2], scale=bn_s[:, 1:2]).then_inc(read["conv2"], 1)
                elif kind == "conv3":
                    oc = f // NH
                    act.wait_ge(read["conv3"], 4 * i + f + 1)
                    nc.scalar.activation(y[:, f % 2, :], y[:, f % 2, :], ACT.Relu, bias=bn_c[:, 2 + oc:3 + oc]).then_inc(y_ready, 1)

            def normalise(i):
                act.wait_ge(aff, 3 * i + 3)
                for c in range(CC):
                    nc.scalar.activation(xin[:, c, :], xin[:, c, :], ACT.Identity, bias=gbi[:, c:c + 1],
                                         scale=gsc[:, c:c + 1]).then_inc(xn_ready, 1)

            act.wait_ge(dve_set, DVE_SET)
            normalise(0)
            for kind, i, f in PROLOGUE:
                job(kind, i, f)
            exps(0, 0)

            def section(i, first, last):
                for s in range(STEPS):
                    if s % KT == 0:
                        if s:
                            save_o(i, s // KT - 1)
                        elif not first:
                            save_o(i - 1, BLOCKS - 1)
                    if s < STEPS - 1:
                        exps(i, s + 1)
                    elif not last:
                        exps(i + 1, 0)
                    if s == NORM_STEP and not last:
                        normalise(i + 1)
                    for kind, di, f in jobs_of(s, first, last):
                        job(kind, i + di, f)

            sections(act, section)
            save_o(B - 1, BLOCKS - 1)
            for kind, _, f in EPILOGUE:
                job(kind, B - 1, f)

        @block.vector
        def _(dve):
            def stats(i, c):
                dve.wait_ge(xin_loaded, 16 * i + 16)
                for hf in range(NH):
                    last = nc.vector.bn_stats(bst[:, c, 2 * hf:2 * hf + 2, :].rearrange("p s k -> p (s k)"), xin[:, c, px(hf)])
                last.then_inc(stats_ready, 1)

            def affine(i):
                dve.wait_ge(rs_ready, i + 1)
                nc.vector.tensor_tensor(gsc[:, :], grs[:, :], vec[:, V_GNW:V_GNW + CC], ALU.mult).then_inc(aff, 1)
                dve.wait_ge(aff, 3 * i + 1)
                nc.vector.tensor_tensor(gms[:, :], gsum[:, :, 1], gsc[:, :], ALU.mult).then_inc(aff, 1)
                dve.wait_ge(aff, 3 * i + 2)
                nc.vector.tensor_tensor(gbi[:, :], vec[:, V_GNB:V_GNB + CC], gms[:, :], ALU.subtract).then_inc(aff, 1)

            def split_x(i, c):
                dve.wait_ge(xn_ready, 2 * i + c + 1)
                wait(dve, filled["qk"], 8 * i)
                nc.vector.tensor_copy(x_hi[:, c, :], xin[:, c, :]).then_inc(xhi_ready, 1)
                dve.wait_ge(xhi_ready, 2 * i + c + 1)
                nc.vector.tensor_tensor(x_lo[:, c, :], xin[:, c, :], x_hi[:, c, :].bitcast(F32),
                                        ALU.subtract).then_inc(xsplit_ready, 1)

            def max_reduce(i, b, m):
                n = 64 * i + 16 * b + m + 1
                dve.wait_ge(max_filled, n)
                nc.vector.reduce_max(mx[:, m // 2, m % 2:m % 2 + 1], MS[:, m % 2, :], AX.X).then_inc(max_read, 1)
                if m == 15:
                    dve.wait_ge(max_read, n)
                    wait(dve, row_filled, BLOCKS * i + b)
                    nc.vector.tensor_tensor(mx1[:, :], mx[:, :, 0], mx[:, :, 1], ALU.max).then_inc(max_ready, 1)

            def row(i, b):
                dve.wait_ge(row_filled, BLOCKS * i + b + 1)
                wait(dve, rows_loaded, 32 * (BLOCKS * i + b))
                nc.vector.tensor_copy(mrow[:, :], MS[0:2 * QT, 0, 0:P]).then_inc(row_read, 1)

            def job(kind, i, f):
                if kind in ("gna", "gnb", "proj", "router", "conv3"):
                    dve.wait_ge(filled[kind], done(kind, i, f))
                if kind == "gna":
                    nc.vector.reduce_sum(gsum[:, :, :], SB[:, 0:CC * SUBSETS * 3].rearrange("p (c s k) -> p c k s", c=CC, k=3),
                                         AX.X).then_inc(read["gna"], 1)
                    dve.wait_ge(read["gna"], i + 1)
                    for c in range(CC):
                        last = nc.vector.tensor_scalar(gdev[:, c, :], bst[:, c, :, 1], gsum[:, c, 1:2], None, ALU.subtract)
                    last.then_inc(dev_done, 1)
                    nc.vector.tensor_scalar(gvar_in[:, :], gsum[:, :, 2], SUBSETS / N, EPS, ALU.mult, ALU.add).then_inc(gvar_part, 1)
                    dve.wait_ge(dev_done, i + 1)
                    nc.vector.tensor_tensor(gdev2[:, :, :], gdev[:, :, :], gdev[:, :, :], ALU.mult).then_inc(dev2_ready, 1)
                elif kind == "gnb":
                    nc.vector.reduce_sum(gvar_of[:, :], SB[:, 0:CC * SUBSETS].rearrange("p (c s) -> p c s", c=CC),
                                         AX.X).then_inc(read["gnb"], 1)
                    dve.wait_ge(read["gnb"], i + 1)
                    dve.wait_ge(gvar_part, i + 1)
                    nc.vector.tensor_tensor(gvar[:, :], gvar_of[:, :], gvar_in[:, :], ALU.add).then_inc(gvar_ready, 1)
                elif kind == "qk":
                    p, isq, hf = f // 4, f % 4 // 2, f % 2
                    dve.wait_ge(qk_hi, 8 * i + f + 1)
                    hi = Q1 if isq else K1
                    col = V_QKVB + (0 if isq else 2) + p
                    for a in range(2):
                        h = 2 * p + a
                        dst = Q2[own(a), h, px(hf)] if isq else K1[other(a), h, px(hf)]
                        last = nc.vector.scalar_tensor_tensor(
                            out=dst, in0=SB[own(a), :], scalar=vec[own(a), col:col + 1],
                            in1=hi[own(a), h, px(hf)].bitcast(F32), op0=ALU.add, op1=ALU.subtract)
                    last.then_inc(read["qk"], 1)
                elif kind == "z":
                    reciprocal(i, f, 0)
                elif kind == "proj":
                    oc, hf = f // NH, f % NH
                    dve.wait_ge(x2_loaded, 16 * i + 16)
                    nc.vector.scalar_tensor_tensor(out=x2[:, oc, px(hf)], in0=SB[:, :], scalar=pbias[:, oc:oc + 1],
                                                   in1=x2[:, oc, px(hf)], op0=ALU.add, op1=ALU.add,
                                                   accum_out=pool4[:, oc, hf:hf + 1]).then_inc(read["proj"], 1)
                    if f == 3:
                        dve.wait_ge(read["proj"], 4 * i + 4)
                        nc.vector.tensor_tensor(pool2[:, :], pool4[:, :, 0], pool4[:, :, 1], ALU.add).then_inc(pool_done, 1)
                        dve.wait_ge(pool_done, 2 * i + 1)
                        for c in range(CC):
                            last = nc.vector.tensor_scalar(poolb[:, c, :], ones[:, :], pool2[:, c:c + 1], None, ALU.mult)
                        last.then_inc(pool_done, 1)
                elif kind == "router":
                    nc.vector.scalar_tensor_tensor(out=logit[:, :], in0=SB[:, 0:E], scalar=1.0 / N, in1=rbias[:, :],
                                                   op0=ALU.mult, op1=ALU.add).then_inc(read["router"], 1)
                elif kind == "conv3":
                    oc, hf = f // NH, f % NH
                    wait(dve, y_stored[f % 2], 16 * (2 * i + f // 2))
                    nc.vector.scalar_tensor_tensor(out=y[:, f % 2, :], in0=SB[:, :], scalar=bn_s[:, 2 + oc:3 + oc],
                                                   in1=x2[:, oc, px(hf)], op0=ALU.mult, op1=ALU.add).then_inc(read["conv3"], 1)

            def reciprocal(i, f, part):
                cols = slice(part * HALF // 2, (part + 1) * HALF // 2)
                dve.wait_ge(read["z"], 4 * i + f + 1)
                nc.vector.reciprocal(rz[:, f % 2, cols], rz[:, f % 2, cols]).then_inc(rz_ready, 1)

            def normalise_o(i, f):
                reciprocal(i, f, 1)
                dve.wait_ge(rz_ready, 2 * (4 * i + f) + 2)
                dve.wait_ge(o_saved, BLOCKS * i + f + 1)
                wait(dve, filled["proj"], 4 * i)
                nc.vector.tensor_tensor(o[:, f // NH, px(f % NH)], o_raw[:, f % 2, :], rz[:, f % 2, :],
                                        ALU.mult).then_inc(o_norm, 1)

            def gates(i):
                dve.wait_ge(rexp_ready, i + 1)
                nc.vector.tensor_scalar(rden[:, :], rexp[:, :], 1.0, None, ALU.add).then_inc(rw_chain, 1)
                dve.wait_ge(rw_chain, 2 * i + 1)
                nc.vector.reciprocal(rw[:, :], rden[:, :]).then_inc(rw_chain, 1)
                dve.wait_ge(rw_chain, 2 * i + 2)

            def mix_experts(i, e0, e1):
                for e in range(e0, e1):
                    if e == 0:
                        gates(i)
                        wait(dve, filled["conv3"], 4 * i)
                        nc.vector.tensor_scalar(mix[:, :], ex[:, 0, :], rw[:, 0:1], None, ALU.mult).then_inc(mix_chain, 1)
                    else:
                        dve.wait_ge(mix_chain, E * i + e)
                        nc.vector.scalar_tensor_tensor(out=mix[:, :], in0=ex[:, e, :], scalar=rw[:, e:e + 1], in1=mix[:, :],
                                                       op0=ALU.mult, op1=ALU.add).then_inc(mix_chain, 1)
                    if e == E - 1:
                        dve.wait_ge(mix_chain, E * i + E)
                        for hf in range(NH):
                            last = nc.vector.tensor_copy(mix3[own(hf), hf, :], mix[own(hf), M1 + M2:MIX])
                        last.then_inc(mix_ready, 1)

            dve.wait_ge(const_loaded, 16 * LOADS)
            nc.vector.tensor_scalar(bn_var[:, :], vec[:, V_V:V_V + 4], EPS, None, ALU.add).then_inc(dve_set, 1)
            nc.vector.tensor_copy(w_hi[:, :, :], w_stage).then_inc(dve_set, 1)
            dve.wait_ge(dve_set, 2)
            nc.vector.tensor_tensor(w_lo[:, :, :], w_stage, w_hi[:, :, :].bitcast(F32), ALU.subtract).then_inc(dve_set, 1)
            dve.wait_ge(bn_pow, 1)
            nc.vector.tensor_tensor(bn_s[:, :], bn_rs[:, :], vec[:, V_G:V_G + 4], ALU.mult).then_inc(dve_set, 1)
            dve.wait_ge(dve_set, 4)
            nc.vector.tensor_tensor(bn_ms[:, :], bn_s[:, :], vec[:, V_M:V_M + 4], ALU.mult).then_inc(dve_set, 1)
            dve.wait_ge(dve_set, 5)
            nc.vector.tensor_tensor(bn_c[:, :], vec[:, V_B:V_B + 4], bn_ms[:, :], ALU.subtract).then_inc(dve_set, 1)
            dve.wait_ge(bias_filled, 1)
            nc.vector.tensor_tensor(pbias[:, :], MS[:, 0, 0:CC], vec[:, V_PROJB:V_PROJB + CC], ALU.add).then_inc(dve_set, 1)
            for c in range(CC):
                stats(0, c)
            for kind, i, f in PROLOGUE:
                job(kind, i, f)
                if kind == "gnb":
                    affine(0)
                    split_x(0, 0)
                    split_x(0, 1)
            for at in PROLOGUE_FILLS[:16]:
                max_reduce(*at)
            row(0, 0)
            for at in PROLOGUE_FILLS[16:]:
                max_reduce(*at)

            def section(i, first, last):
                mixed = 0
                for s in range(STEPS):
                    fills = fills_at(i, s, last)
                    jobs = jobs_of(s, first, last)
                    if s % KT == ROWSTEP and not (last and s > STEPS - KT):
                        b = s // KT + 1
                        row(i + b // BLOCKS, b % BLOCKS)
                    for at in fills[0:1]:
                        max_reduce(*at)
                    for kind, di, f in jobs[0:1]:
                        job(kind, i + di, f)
                    for at in fills[1:]:
                        max_reduce(*at)
                    for kind, di, f in jobs[1:]:
                        job(kind, i + di, f)
                    for kind, di, f in jobs_of(s - 1, first, last):
                        if kind == "z":
                            normalise_o(i + di, f)
                    if s in STATS_STEPS and not last:
                        stats(i + 1, STATS_STEPS.index(s))
                    if s == AFFINE_STEP and not last:
                        affine(i + 1)
                    if s in SPLIT_STEPS and not last:
                        split_x(i + 1, SPLIT_STEPS.index(s))
                    if s in MIX_STEPS and not first:
                        mix_experts(i - 1, mixed, mixed + MIX_STEPS[s])
                        mixed += MIX_STEPS[s]

            sections(dve, section)
            for kind, _, f in EPILOGUE:
                job(kind, B - 1, f)
                if kind == "z":
                    normalise_o(B - 1, f)
                if kind == "router":
                    mix_experts(B - 1, 0, E)


_ORDER = ["x", "vecs", "router_b", "wqkv", "wproj", "wrouter", "experts", "neg_eye", "group_avg"]


def _chunks(v):
    return np.asarray(v).reshape(-1, P).T


def kernel(**inputs):
    import concourse.bacc as _bacc
    from concourse.bass_utils import run_bass_kernel_spmd as _run

    a = {k: np.asarray(v) for k, v in inputs.items()}
    c1 = {k[len("L1_conv_"):]: v for k, v in a.items() if k.startswith("L1_conv_")}

    def layers(k):
        return np.concatenate([np.tile(c1[k + "1"], 2)[:, None], np.tile(c1[k + "2"], 2)[:, None], _chunks(c1[k + "3"])], axis=1)

    vecs = np.concatenate([_chunks(a["L0_conv_gn_w"]), _chunks(a["L0_conv_gn_b"]), _chunks(a["L0_conv_qkv_b"]),
                           _chunks(a["L0_conv_proj_b"]), layers("g"), layers("b"), layers("m"), layers("v")], axis=1)

    def stationary(w):
        return w.T.reshape(CC, P, -1).transpose(1, 0, 2)

    e1 = c1["w1"][:, :, :, 0, 0].transpose(2, 0, 1).reshape(CC, P, E, WID).transpose(1, 2, 0, 3).reshape(P, E, M1)
    w2 = c1["w2"].transpose(4, 2, 0, 3, 1)
    low = np.concatenate([w2[0], w2[2]], axis=2)
    high = np.concatenate([w2[1], np.zeros_like(w2[1])], axis=2)
    e2 = np.concatenate([low, high], axis=0).reshape(P, E, M2)
    w3 = c1["w3"][:, :, :, 0, 0].transpose(2, 0, 1)
    e3 = np.concatenate([w3, w3], axis=0)
    arrays = {
        "x": a["x"].reshape(B, CC, P, N),
        "vecs": vecs,
        "router_b": np.broadcast_to(c1["router_b"], (P, E)),
        "wqkv": stationary(a["L0_conv_qkv_w"]),
        "wproj": stationary(a["L0_conv_proj_w"]),
        "wrouter": stationary(c1["router_w"]),
        "experts": np.concatenate([e1, e2, e3], axis=2),
        "neg_eye": -np.eye(P, dtype=np.float32),
        "group_avg": np.kron(np.eye(P // GROUP, dtype=np.float32), np.full((GROUP, GROUP), 1 / (GROUP * SUBSETS), np.float32)),
    }
    nc = _bacc.Bacc("TRN2", target_bir_lowering=False, num_devices=1)
    data, args = {}, []
    for name in _ORDER:
        v = np.ascontiguousarray(arrays[name])
        data[f"in_{name}_dram"] = v
        ap = nc.dram_tensor(f"in_{name}_dram", v.shape, mybir.dt.from_np(v.dtype), kind="ExternalInput").ap()
        args.append(ap.rearrange("b c p n -> b p c n") if name == "x" else ap)
    res = nc.dram_tensor("out_0_dram", (B, CC, P, N), F32, kind="ExternalOutput").ap()
    build(nc, *args, res.rearrange("b c p n -> b p c n"))
    r = _run(nc, [data], core_ids=[0])
    return r.results[0]["out_0_dram"].reshape(B, C, H, W)
```

```python
from contextlib import ExitStack

import numpy as np

import concourse.bass as bass
from concourse import mybir

F32 = mybir.dt.float32
F32R = mybir.dt.float32r
ALU = mybir.AluOpType
ACT = mybir.ActivationFunctionType
AX = mybir.AxisListType

B, C, H, W = 16, 256, 32, 32
N = H * W
P = 128
CC = C // P
HEADS, D = 4, 64
PAIRS = HEADS // 2
HALF = 512
NH = N // HALF
KT = N // P
QT = HALF // P
BLOCKS = PAIRS * NH
STEPS = BLOCKS * KT
GROUP = 8
SUBSETS = 2 * NH
E = 8
WID = 64
EPS = 1e-5
PW = W + 2
PAD = (H + 2) * PW
TAPS = 6
M1, M2, M3 = CC * WID, TAPS * WID, C
MIX = M1 + M2 + M3
YBUF = 3
PBUF = 4

V_GNW, V_GNB, V_QKVB, V_PROJB, V_G, V_B, V_M, V_V = 0, 2, 4, 10, 12, 16, 20, 24
VECS = 28

SIDE = {
    0: [None, ("z", -1, 3)], 1: [("qk", 0, 5)], 2: [("qk", 0, 6)], 3: [("qk", 0, 7)], 4: [("proj", -1, 0)],
    5: [("proj", -1, 1), ("row", 0, 1)], 6: [("proj", -1, 2)], 7: [("proj", -1, 3)], 8: [("router", -1, 0)],
    9: [("gna", 1, 0)], 10: [("gnb", 1, 0)], 11: [("z", 0, 0)], 13: [None, ("row", 0, 2)],
    15: [("qk", 1, 0)], 16: [("qk", 1, 1)], 17: [("qk", 1, 2)], 18: [("qk", 1, 3)], 19: [("conv1", -1, 0)],
    20: [("v", 1, 0)], 21: [("v", 1, 1), ("row", 0, 3)], 22: [("conv2a", -1, 0)], 23: [("conv2", -1, 0)],
    24: [("z", 0, 1)], 25: [("conv3", -1, 0)], 26: [("v", 1, 2)], 27: [("conv3", -1, 1)], 28: [("z", 0, 2)],
    29: [("conv3", -1, 2), ("row", 1, 0)], 30: [("v", 1, 3), ("conv3", -1, 3)], 31: [("qk", 1, 4)],
}
NORMALISE = {1: (-1, 3), 20: (0, 0), 24: (0, 1), 30: (0, 2)}
PROLOGUE = [("gna", 0, 0), ("gnb", 0, 0)] + [("qk", 0, f) for f in range(4)] + [("v", 0, f) for f in range(4)] + [("qk", 0, 4)]
EPILOGUE = ([("z", 0, 3)] + [("proj", 0, f) for f in range(4)] + [("router", 0, 0), ("conv1", 0, 0),
            ("conv2a", 0, 0), ("conv2", 0, 0)] + [("conv3", 0, f) for f in range(4)])
FILLS_AHEAD = 6
FILLS = [2, 1, 1, 3, 3, 3, 2, 3, 2, 2, 1, 1, 2, 1, 1, 3, 2, 3, 2, 2, 2, 2, 2, 2, 2, 2, 2, 2, 2, 3, 2, 1]
STATS_STEPS, AFFINE_STEP, NORM_STEPS, SPLIT_STEPS = (4, 5), 11, (11, 12), (13, 14)
MIX_STEPS = {9: 2, 10: 2, 11: 2, 12: 1, 13: 1}


def build(nc, x, vecs, router_b, wqkv, wproj, wrouter, experts, neg_eye, group_avg, out):
    ctx = ExitStack()
    with ctx:
        def sb(name, shape, dt=F32):
            return ctx.enter_context(nc.sbuf_tensor(name, shape, dt))

        def pb(name, shape):
            return ctx.enter_context(nc.psum_tensor(name, shape, F32))

        def sem(name):
            return ctx.enter_context(nc.semaphore(name))

        vec = sb("vec", [P, VECS])
        rbias = sb("rbias", [P, E])
        w_hi = sb("w_hi", [P, CC, 3 * C], F32R)
        w_lo = sb("w_lo", [P, CC, 3 * C], F32R)
        wp = sb("wp", [P, CC, C])
        wr = sb("wr", [P, CC, E])
        ex = sb("ex", [P, E, MIX])
        negeye = sb("negeye", [P, P])
        gavg = sb("gavg", [P, P])
        ones = sb("ones", [P, P])
        neghalf = sb("neghalf", [P, 4])
        pbias = sb("pbias", [P, CC])
        bn_var = sb("bn_var", [P, 4])
        bn_rs = sb("bn_rs", [P, 4])
        bn_s = sb("bn_s", [P, 4])
        bn_ms = sb("bn_ms", [P, 4])
        bn_c = sb("bn_c", [P, 4])
        xin = sb("xin", [P, CC, N])
        x_hi = sb("x_hi", [P, CC, N], F32R)
        x_lo = sb("x_lo", [P, CC, N], F32R)
        Q1 = sb("Q1", [P, HEADS, N], F32R)
        Q2 = sb("Q2", [P, HEADS, N], F32R)
        K1 = sb("K1", [P, HEADS, N], F32R)
        K2 = sb("K2", [P, HEADS, N], F32R)
        V = sb("V", [P, PAIRS, KT, P])
        v_next = sb("v_next", [P, KT, P])
        prob = sb("prob", [P, PBUF, 2, HALF])
        w_stage = prob[:, :, :, :].rearrange("p b a n -> p (b a n)")[:, 0:CC * 3 * C].rearrange("p (c n) -> p c n", c=CC)
        psum_p = sb("psum_p", [P, 2, 2, HALF])
        o_raw = sb("o_raw", [P, 2, HALF])
        rz = sb("rz", [P, 2, HALF])
        o = sb("o", [P, CC, N])
        x2 = sb("x2", [P, CC, N])
        hpad = sb("hpad", [P, PAD + 2])
        h2 = sb("h2", [P, HALF])
        y = sb("y", [P, YBUF, HALF])
        mix = sb("mix", [P, MIX])
        mix3 = sb("mix3", [P, NH, C])
        mx = sb("mx", [P, 2, 2 * QT, NH])
        mx1 = sb("mx1", [P, 2 * QT])
        mrow = sb("mrow", [2 * QT, P], F32R)
        bst = sb("bst", [P, CC, SUBSETS, 3])
        gsum = sb("gsum", [P, CC, 3])
        gdev = sb("gdev", [P, CC, SUBSETS])
        gdev2 = sb("gdev2", [P, CC, SUBSETS])
        gvar_in = sb("gvar_in", [P, CC])
        gvar_of = sb("gvar_of", [P, CC])
        gvar = sb("gvar", [P, CC])
        grs = sb("grs", [P, CC])
        gsc = sb("gsc", [P, CC])
        gms = sb("gms", [P, CC])
        gbi = sb("gbi", [P, CC])
        pool4 = sb("pool4", [P, CC, NH])
        pool2 = sb("pool2", [P, CC])
        poolb = sb("poolb", [P, CC, P])
        logit = sb("logit", [P, E])
        rexp = sb("rexp", [P, E])
        rden = sb("rden", [P, E])
        rw = sb("rw", [P, E])

        S = pb("S", [P, 2, 2, HALF])
        MS = pb("MS", [P, 2, HALF])
        PV = pb("PV", [P, HALF])
        SB = pb("SB", [P, HALF])

        const_loaded = sem("const_loaded")
        consts_set = sem("consts_set")
        dve_set = sem("dve_set")
        bias_filled = sem("bias_filled")
        bn_pow = sem("bn_pow")
        xin_loaded = sem("xin_loaded")
        x2_loaded = sem("x2_loaded")
        v1_loaded = sem("v1_loaded")
        rows_loaded = sem("rows_loaded")
        dup_loaded = [sem(f"dup{n}_loaded") for n in range(PAIRS)]
        y_stored = [sem(f"y{f}_stored") for f in range(4)]
        s_done = sem("s_done")
        exp_done = sem("exp_done")
        pv_done = sem("pv_done")
        add_done = sem("add_done")
        o_saved = sem("o_saved")
        o_norm = sem("o_norm")
        rz_ready = sem("rz_ready")
        max_filled = sem("max_filled")
        max_read = sem("max_read")
        max_ready = sem("max_ready")
        h_saved = sem("h_saved")
        filled = {k: sem(k + "_filled") for k in ("qk", "v", "z", "proj", "gna", "gnb", "router", "conv1", "conv2", "conv3", "row")}
        read = {k: sem(k + "_read") for k in ("qk", "v", "z", "proj", "gna", "gnb", "router", "conv1", "conv2", "conv3", "row")}
        per_image = {"row": BLOCKS, "qk": 8, "v": 4, "z": 4, "proj": 4, "gna": 1, "gnb": 1, "router": 1, "conv1": 1, "conv2": 1, "conv3": 4}
        qk_hi = sem("qk_hi")
        stats_ready = sem("stats_ready")
        gvar_part = sem("gvar_part")
        gvar_ready = sem("gvar_ready")
        dev_done = sem("dev_done")
        dev2_ready = sem("dev2_ready")
        rs_ready = sem("rs_ready")
        aff = sem("aff")
        xn_ready = sem("xn_ready")
        xsplit_ready = sem("xsplit_ready")
        pool_done = sem("pool_done")
        rexp_ready = sem("rexp_ready")
        rw_chain = sem("rw_chain")
        mix_chain = sem("mix_chain")
        mix_ready = sem("mix_ready")
        y_ready = sem("y_ready")

        LOADS, DVE_SET, CONSTS_SET = 8, 7, 4 + 3 * HEADS

        block = ctx.enter_context(nc.Block())

        def wait(eng, s, value):
            if not isinstance(value, int) or value > 0:
                eng.wait_ge(s, value)

        def adds_reading(g_image, s):
            return g_image * (STEPS - BLOCKS) + (s // KT) * (KT - 1) + max(1, s % KT)

        def done(kind, i, f):
            return per_image[kind] * i + f + 1

        def jobs_of(s, first, last):
            gone = {-1} if first else set()
            gone |= {1} if last else set()
            return [j for j in SIDE.get(s, []) if j and j[1] not in gone]

        def sections(eng, section):
            section(0, True, False)
            section(1, False, False)
            with eng.Fori(2, B - 1) as i:
                section(i, False, False)
            section(B - 1, False, True)

        def is_second(s, job):
            return SIDE[s].index(job) == 1

        def fills_at(i, s, last):
            first_fill = 16 + FILLS_AHEAD + sum(FILLS[:s])
            fills = [divmod(n, 16) for n in range(first_fill, first_fill + FILLS[s])]
            return [(i + b // BLOCKS, b % BLOCKS, m) for b, m in fills if not (last and b >= BLOCKS)]

        PROLOGUE_FILLS = [(0, 0, m) for m in range(16)] + [(0, 1, m) for m in range(FILLS_AHEAD)]

        def own(a):
            return slice(64 * a, 64 * a + 64)

        def other(a):
            return slice(64 - 64 * a, 128 - 64 * a)

        def px(hf):
            return slice(hf * HALF, hf * HALF + HALF)

        @block.sync
        def _(sp):
            def load_xin(i):
                if not isinstance(i, int) or i > 0:
                    wait(sp, xsplit_ready, 2 * i)
                sp.dma_start(xin[:, :, :], x[i]).then_inc(xin_loaded, 16)

            def load_x2(i):
                wait(sp, read["conv3"], 4 * i)
                sp.dma_start(x2[:, :, :], x[i]).then_inc(x2_loaded, 16)

            def load_v1(i):
                sp.wait_ge(pv_done, STEPS * i + 1)
                sp.dma_start(V[:, 1, :, :], v_next[:, :, :]).then_inc(v1_loaded, 16)

            def dup(i, f):
                p, kind, hf = f // 4, f % 4 // 2, f % 2
                for a in range(2):
                    sp.wait_ge(qk_hi, 2 * (8 * i + f) + a + 1)
                    h = 2 * p + a
                    if kind:
                        src, dst = Q1[own(a), h, px(hf)], Q1[other(a), h, px(hf)]
                    else:
                        src, dst = K1[own(a), h, px(hf)], K2[own(a), h, px(hf)]
                    sp.dma_start(dst.bitcast(F32), src.bitcast(F32)).then_inc(dup_loaded[p], 16)

            def rows(i, b):
                p, hf = b // NH, b % NH
                sp.wait_ge(read["row"], BLOCKS * i + b + 1)
                for a in range(2):
                    r = 64 - 64 * a
                    sp.dma_start(Q2[r:r + 1, 2 * p + a, px(hf)].bitcast(F32),
                                 mrow[QT * a:QT * a + QT, :].bitcast(F32)).then_inc(rows_loaded, 16)

            def shift_h(i):
                sp.wait_ge(read["conv1"], i + 1)
                sp.dma_start(hpad[64:128, 0:PAD], hpad[0:64, 1:PAD + 1]).then_inc(h_saved, 16)

            def store(i, f):
                oc, hf = f // NH, f % NH
                wait(sp, y_ready, 4 * i + f + 1)
                sp.dma_start(out[i, :, oc, px(hf)], y[:, f % YBUF, :]).then_inc(y_stored[f], 16)

            def section(i, first, last):
                load_v1(i)
                for s in range(STEPS):
                    for kind, di, f in jobs_of(s, first, last):
                        if kind == "qk":
                            dup(i + di, f)
                        if kind == "row":
                            rows(i + di, f)
                        if kind == "conv1":
                            shift_h(i + di)
                        if kind == "conv3":
                            store(i + di, f)
                    if s == STEPS - 1:
                        load_x2(i)
                    if s == 0 and not last:
                        load_xin(i + 1)

            sp.dma_start(vec[:, :], vecs).then_inc(const_loaded, 16)
            load_xin(0)
            sp.dma_start(w_stage, wqkv).then_inc(const_loaded, 16)
            sp.dma_start(gavg[:, :], group_avg).then_inc(const_loaded, 16)
            sp.dma_start(negeye[:, :], neg_eye).then_inc(const_loaded, 16)
            sp.dma_start(wp[:, :, :], wproj).then_inc(const_loaded, 16)
            sp.dma_start(wr[:, :, :], wrouter).then_inc(const_loaded, 16)
            sp.dma_start(rbias[:, :], router_b).then_inc(const_loaded, 16)
            sp.dma_start(ex[:, :, :], experts).then_inc(const_loaded, 16)
            for f in range(5):
                dup(0, f)
            rows(0, 0)
            sections(sp, section)
            shift_h(B - 1)
            for f in range(4):
                store(B - 1, f)
            for f in range(4):
                sp.wait_ge(y_stored[f], 16 * B)

        @block.gpsimd
        def _(pool):
            count = 0
            fills = [(neghalf[:, :], -0.5), (ones[:, :], 1.0), (hpad[:, :], 0.0), (mix3[:, :, :], 0.0)]
            for h in range(HEADS):
                r = 64 - 64 * (h % 2)
                fills += [(t[other(h % 2), h, :].bitcast(F32), 0.0) for t in (Q2, K2)]
                fills += [(K2[r:r + 1, h, :].bitcast(F32), 1.0)]
            for dst, value in fills:
                nc.gpsimd.memset(dst, value).then_inc(consts_set, 1)
                count += 1
                pool.wait_ge(consts_set, count)
            pool.wait_ge(dve_set, 1)
            nc.gpsimd.tensor_tensor(bn_rs[:, :], bn_var[:, :], neghalf[:, :], ALU.pow).then_inc(bn_pow, 1)

            def rstd(i):
                pool.wait_ge(gvar_ready, i + 1)
                nc.gpsimd.tensor_tensor(grs[:, :], gvar[:, :], neghalf[:, 0:CC], ALU.pow).then_inc(rs_ready, 1)

            def section(i, first, last):
                for s in range(STEPS):
                    b, j = s // KT, s % KT
                    acc = psum_p[:, b % 2, :, :]
                    if j == 1:
                        wait(pool, filled["z"], BLOCKS * i + b - 1)
                    if j > 0:
                        pool.wait_ge(exp_done, STEPS * i + s + 1)
                        if j > 1:
                            pool.wait_ge(add_done, adds_reading(i, s) - 1)
                        first_in = prob[:, (s - 1) % PBUF, :, :] if j == 1 else acc
                        nc.gpsimd.tensor_tensor(acc, first_in, prob[:, s % PBUF, :, :], ALU.add).then_inc(add_done, 1)
                    if s == AFFINE_STEP - 1 and not last:
                        rstd(i + 1)

            rstd(0)
            sections(pool, section)

        @block.tensor
        def _(pe):
            def split_mm(dst, wl, xl, pairs):
                k = 0
                for c in range(CC):
                    for w, m in pairs:
                        last = nc.tensor.matmul(dst, wl(w, c), xl(m, c), start=(k == 0), stop=(k == 3 * CC - 1))
                        k += 1
                return last

            def job(kind, i, f, before):
                for k, bi, bf in before:
                    pe.wait_ge(read[k], done(k, bi, bf))
                if kind == "gna":
                    pe.wait_ge(stats_ready, CC * i + CC)
                    last = nc.tensor.matmul(SB[:, 0:CC * SUBSETS * 3], gavg[:, :], bst[:, :, :, :].rearrange("p c s k -> p (c s k)"), start=True, stop=True)
                elif kind == "gnb":
                    pe.wait_ge(dev2_ready, i + 1)
                    last = nc.tensor.matmul(SB[:, 0:CC * SUBSETS], gavg[:, :], gdev2[:, :, :].rearrange("p c s -> p (c s)"), start=True, stop=True)
                elif kind == "qk":
                    p, isq, hf = f // 4, f % 4 // 2, f % 2
                    if f == 0:
                        pe.wait_ge(xsplit_ready, 2 * i + 2)
                    col = (0 if isq else C) + p * P
                    last = split_mm(SB[:, :], lambda w, c: w[:, c, col:col + P], lambda m, c: m[:, c, px(hf)],
                                    ((w_hi, x_hi), (w_hi, x_lo), (w_lo, x_hi)))
                elif kind == "v":
                    for t in (0, 1):
                        kt = 2 * f + t
                        last = split_mm(SB[:, t * C:t * C + C], lambda w, c: w[:, c, kt * P:kt * P + P],
                                        lambda m, c: m[:, c, 2 * C:3 * C], ((x_hi, w_hi), (x_lo, w_hi), (x_hi, w_lo)))
                elif kind == "z":
                    pe.wait_ge(add_done, adds_reading(i, KT * f + KT - 1))
                    for a in range(2):
                        last = nc.tensor.matmul(SB[own(a), :], ones[:, 0:D], psum_p[:, f % 2, a, :], start=True, stop=True)
                elif kind == "proj":
                    oc, hf = f // NH, f % NH
                    if f == 0:
                        pe.wait_ge(o_norm, BLOCKS * i + BLOCKS)
                    for c in range(CC):
                        last = nc.tensor.matmul(SB[:, :], wp[:, c, oc * P:oc * P + P], o[:, c, px(hf)],
                                                start=(c == 0), stop=(c == CC - 1))
                elif kind == "row":
                    pe.wait_ge(max_ready, BLOCKS * i + f + 1)
                    last = nc.tensor.matmul(SB[0:2 * QT, 0:P], mx1[:, :], negeye[:, :], start=True, stop=True)
                elif kind == "router":
                    pe.wait_ge(pool_done, 2 * i + 2)
                    for c in range(CC):
                        last = nc.tensor.matmul(SB[:, 0:E], poolb[:, c, :], wr[:, c, :], start=(c == 0), stop=(c == CC - 1))
                elif kind == "conv1":
                    pe.wait_ge(mix_ready, i + 1)
                    for c in range(CC):
                        for hf in range(NH):
                            last = nc.tensor.matmul(SB[own(hf), :], mix[:, c * WID:c * WID + WID], x2[:, c, px(hf)],
                                                    start=(c == 0), stop=(c == CC - 1))
                elif kind in ("conv2a", "conv2"):
                    if kind == "conv2a":
                        pe.wait_ge(h_saved, 16 * i + 16)
                    rows_hf = H // NH
                    for tap in (range(3) if kind == "conv2a" else range(3, 6)):
                        dy, dx = tap % 3, 2 * (tap // 3)
                        for hf in range(NH):
                            at = (dy + hf * rows_hf) * PW + dx
                            src = hpad[:, at:at + rows_hf * PW].rearrange("p (r w) -> p r w", w=PW)[:, :, 0:W]
                            last = nc.tensor.matmul(SB[own(hf), :], mix[:, M1 + tap * WID:M1 + tap * WID + WID], src,
                                                    start=(tap == 0), stop=(tap == TAPS - 1))
                elif kind == "conv3":
                    oc, hf = f // NH, f % NH
                    if f == 0:
                        pe.wait_ge(read["conv2"], i + 1)
                    last = nc.tensor.matmul(SB[:, :], mix3[:, hf, oc * P:oc * P + P], h2[:, :], start=True, stop=True)
                if kind != "conv2a":
                    last.then_inc(filled[kind], 1)

            def max_fill(i, b, m):
                p, hf, a, t, nh = b // NH, b % NH, m // (2 * QT), m // 2 % QT, m % 2
                h = 2 * p + a
                if m == 0:
                    pe.wait_ge(read["qk"], 8 * i + 4 * p + 4)
                    pe.wait_ge(dup_loaded[p], 32 * 4 * (i + 1))
                wait(pe, max_read, 64 * i + 16 * b + m - 1)
                q0 = hf * HALF + t * P
                nc.tensor.matmul(MS[:, m % 2, :], Q1[:, h, q0:q0 + P], K1[:, h, px(nh)],
                                 start=True, stop=True).then_inc(max_filled, 1)

            def scores(i, s):
                b, kt = s // KT, s % KT
                p, hf = b // NH, b % NH
                wait(pe, exp_done, STEPS * i + s - 1)
                for a in range(2):
                    h = 2 * p + a
                    nc.tensor.matmul(S[:, s % 2, a, :], K1[:, h, kt * P:kt * P + P], Q1[:, h, px(hf)], start=True, stop=False)
                    if kt == 0 and a == 0:
                        pe.wait_ge(rows_loaded, 32 * (BLOCKS * i + b + 1))
                    last = nc.tensor.matmul(S[:, s % 2, a, :], K2[:, h, kt * P:kt * P + P], Q2[:, h, px(hf)], start=False, stop=True)
                last.then_inc(s_done, 1)

            def pv(i, s):
                b, kt = s // KT, s % KT
                if s == 0:
                    pe.wait_ge(read["v"], 4 * i + 4)
                if s == KT * NH:
                    pe.wait_ge(v1_loaded, 16 * i + 16)
                if kt == 0:
                    wait(pe, o_saved, BLOCKS * i + b)
                pe.wait_ge(exp_done, STEPS * i + s + 1)
                for a in range(2):
                    last = nc.tensor.matmul(PV[own(a), :], V[:, b // NH, kt, a * D:a * D + D], prob[:, s % PBUF, a, :],
                                            start=(kt == 0), stop=(kt == KT - 1))
                last.then_inc(pv_done, 1)

            pe.wait_ge(const_loaded, 16 * LOADS)
            for oc in range(CC):
                for c in range(CC):
                    last = nc.tensor.matmul(MS[:, 0, oc:oc + 1], wp[:, c, oc * P:oc * P + P], vec[:, V_QKVB + 4 + c:V_QKVB + 5 + c],
                                            start=(c == 0), stop=(c == CC - 1))
            last.then_inc(bias_filled, 1)
            pe.wait_ge(consts_set, CONSTS_SET)
            before = []
            for kind, i, f in PROLOGUE:
                job(kind, i, f, before)
                before = [(kind, i, f)]
            pe.wait_ge(dve_set, DVE_SET)
            for at in PROLOGUE_FILLS[:16]:
                max_fill(*at)
            job("row", 0, 0, before)
            for at in PROLOGUE_FILLS[16:]:
                max_fill(*at)
            scores(0, 0)

            def section(i, first, last):
                held = [("row", 0, 0)] if first else [("qk", i, 4)]
                for s in range(STEPS):
                    fills = fills_at(i, s, last)
                    jobs = jobs_of(s, first, last)
                    if s < STEPS - 1:
                        scores(i, s + 1)
                    elif not last:
                        scores(i + 1, 0)
                    for at in fills[0:1]:
                        max_fill(*at)
                    for second in (False, True):
                        for j in jobs:
                            if is_second(s, j) == second:
                                kind, di, f = j
                                job(kind, i + di, f, [] if kind == "conv2" else held)
                                held = [(kind, i + di, f)]
                        if not second:
                            for at in fills[1:2]:
                                max_fill(*at)
                            pv(i, s)
                            for at in fills[2:]:
                                max_fill(*at)

            sections(pe, section)
            held = [("conv3", B - 2, 3)]
            for kind, _, f in EPILOGUE:
                job(kind, B - 1, f, [] if kind == "conv2" else held)
                held = [(kind, B - 1, f)]

        @block.scalar
        def _(act):
            def exps(i, s):
                wait(act, pv_done, STEPS * i + s - PBUF + 1)
                wait(act, add_done, adds_reading(i, s - PBUF) if s >= PBUF else
                     (adds_reading(i - 1, STEPS + s - PBUF) if not isinstance(i, int) or i > 0 else 0))
                act.wait_ge(s_done, STEPS * i + s + 1)
                nc.scalar.activation(prob[:, s % PBUF, :, :], S[:, s % 2, :, :], ACT.Exp, scale=D ** -0.5).then_inc(exp_done, 1)

            def save_o(i, b):
                act.wait_ge(pv_done, STEPS * i + KT * b + KT)
                wait(act, o_norm, BLOCKS * i + b - 1)
                nc.scalar.activation(o_raw[:, b % 2, :], PV[:, :], ACT.Copy).then_inc(o_saved, 1)

            def job(kind, i, f):
                if kind == "qk":
                    p, isq, hf = f // 4, f % 4 // 2, f % 2
                    act.wait_ge(filled["qk"], 8 * i + f + 1)
                    wait(act, s_done, STEPS * (i - 1) + KT * NH * (p + 1))
                    dst = Q1 if isq else K1
                    col = V_QKVB + (0 if isq else 2) + p
                    for a in range(2):
                        nc.scalar.activation(dst[own(a), 2 * p + a, px(hf)], SB[own(a), :], ACT.Identity,
                                             bias=vec[own(a), col:col + 1]).then_inc(qk_hi, 1)
                elif kind == "v":
                    act.wait_ge(filled["v"], 4 * i + f + 1)
                    wait(act, pv_done, STEPS * (i - 1) + KT * NH)
                    wait(act, v1_loaded, 16 * i)
                    src = SB[:, :].rearrange("p (t q n) -> p t q n", t=2, q=PAIRS)
                    nc.scalar.activation(V[:, 0, 2 * f:2 * f + 2, :], src[:, :, 0, :], ACT.Copy)
                    nc.scalar.activation(v_next[:, 2 * f:2 * f + 2, :], src[:, :, 1, :], ACT.Copy).then_inc(read["v"], 1)
                elif kind == "z":
                    act.wait_ge(filled["z"], 4 * i + f + 1)
                    wait(act, o_norm, 4 * i + f - 1)
                    nc.scalar.activation(rz[:, f % 2, :], SB[:, :], ACT.Copy).then_inc(read["z"], 1)
                elif kind == "router":
                    act.wait_ge(read["router"], i + 1)
                    nc.scalar.activation(rexp[:, :], logit[:, :], ACT.Exp, scale=-1.0).then_inc(rexp_ready, 1)
                elif kind == "conv1":
                    act.wait_ge(filled["conv1"], i + 1)
                    rows_hf = H // NH
                    for hf in range(NH):
                        at = (1 + hf * rows_hf) * PW + 1
                        dst = hpad[0:64, at:at + rows_hf * PW].rearrange("p (r w) -> p r w", w=PW)[:, :, 0:W]
                        src = SB[own(hf), :].rearrange("p (r w) -> p r w", w=W)
                        last = nc.scalar.activation(dst, src, ACT.Relu, bias=bn_c[own(hf), 0:1], scale=bn_s[own(hf), 0:1])
                    last.then_inc(read["conv1"], 1)
                elif kind == "conv2":
                    act.wait_ge(filled["conv2"], i + 1)
                    nc.scalar.activation(h2[:, :], SB[:, :], ACT.Relu, bias=bn_c[:, 1:2], scale=bn_s[:, 1:2]).then_inc(read["conv2"], 1)
                elif kind == "conv3":
                    oc = f // NH
                    act.wait_ge(read["conv3"], 4 * i + f + 1)
                    nc.scalar.activation(y[:, f % YBUF, :], y[:, f % YBUF, :], ACT.Relu, bias=bn_c[:, 2 + oc:3 + oc]).then_inc(y_ready, 1)

            def normalise(i, c):
                if c == 0:
                    act.wait_ge(aff, 3 * i + 3)
                    wait(act, filled["qk"], 8 * i)
                nc.scalar.activation(x_hi[:, c, :], xin[:, c, :], ACT.Identity, bias=gbi[:, c:c + 1], scale=gsc[:, c:c + 1])
                nc.scalar.activation(xin[:, c, :], xin[:, c, :], ACT.Identity, bias=gbi[:, c:c + 1],
                                     scale=gsc[:, c:c + 1]).then_inc(xn_ready, 1)

            act.wait_ge(dve_set, DVE_SET)
            for c in range(CC):
                normalise(0, c)
            for kind, i, f in PROLOGUE:
                job(kind, i, f)
            exps(0, 0)

            def section(i, first, last):
                for s in range(STEPS):
                    if s % KT == 0:
                        if s:
                            save_o(i, s // KT - 1)
                        elif not first:
                            save_o(i - 1, BLOCKS - 1)
                    if s < STEPS - 1:
                        exps(i, s + 1)
                    elif not last:
                        exps(i + 1, 0)
                    for kind, di, f in jobs_of(s, first, last):
                        job(kind, i + di, f)
                    if s in NORM_STEPS and not last:
                        normalise(i + 1, NORM_STEPS.index(s))

            sections(act, section)
            save_o(B - 1, BLOCKS - 1)
            for kind, _, f in EPILOGUE:
                job(kind, B - 1, f)

        @block.vector
        def _(dve):
            def stats(i, c):
                dve.wait_ge(xin_loaded, 16 * i + 16)
                for hf in range(NH):
                    last = nc.vector.bn_stats(bst[:, c, 2 * hf:2 * hf + 2, :].rearrange("p s k -> p (s k)"), xin[:, c, px(hf)])
                last.then_inc(stats_ready, 1)

            def affine(i):
                dve.wait_ge(rs_ready, i + 1)
                nc.vector.tensor_tensor(gsc[:, :], grs[:, :], vec[:, V_GNW:V_GNW + CC], ALU.mult).then_inc(aff, 1)
                dve.wait_ge(aff, 3 * i + 1)
                nc.vector.tensor_tensor(gms[:, :], gsum[:, :, 1], gsc[:, :], ALU.mult).then_inc(aff, 1)
                dve.wait_ge(aff, 3 * i + 2)
                nc.vector.tensor_tensor(gbi[:, :], vec[:, V_GNB:V_GNB + CC], gms[:, :], ALU.subtract).then_inc(aff, 1)

            def split_x(i, c):
                dve.wait_ge(xn_ready, 2 * i + c + 1)
                wait(dve, filled["qk"], 8 * i)
                nc.vector.tensor_tensor(x_lo[:, c, :], xin[:, c, :], x_hi[:, c, :].bitcast(F32),
                                        ALU.subtract).then_inc(xsplit_ready, 1)

            def max_reduce(i, b, m):
                n = 64 * i + 16 * b + m + 1
                dve.wait_ge(max_filled, n)
                nc.vector.reduce_max(mx[:, b % 2, m // 2, m % 2:m % 2 + 1], MS[:, m % 2, :], AX.X).then_inc(max_read, 1)
                if m == 15:
                    dve.wait_ge(max_read, n)
                    wait(dve, filled["row"], BLOCKS * i + b)
                    nc.vector.tensor_tensor(mx1[:, :], mx[:, b % 2, :, 0], mx[:, b % 2, :, 1], ALU.max).then_inc(max_ready, 1)

            def row(i, b):
                wait(dve, rows_loaded, 32 * (BLOCKS * i + b))
                nc.vector.tensor_copy(mrow[:, :], SB[0:2 * QT, 0:P]).then_inc(read["row"], 1)

            def job(kind, i, f):
                if kind in ("gna", "gnb", "proj", "router", "conv3", "row"):
                    dve.wait_ge(filled[kind], done(kind, i, f))
                if kind == "gna":
                    nc.vector.reduce_sum(gsum[:, :, :], SB[:, 0:CC * SUBSETS * 3].rearrange("p (c s k) -> p c k s", c=CC, k=3),
                                         AX.X).then_inc(read["gna"], 1)
                    dve.wait_ge(read["gna"], i + 1)
                    for c in range(CC):
                        last = nc.vector.tensor_scalar(gdev[:, c, :], bst[:, c, :, 1], gsum[:, c, 1:2], None, ALU.subtract)
                    last.then_inc(dev_done, 1)
                    nc.vector.tensor_scalar(gvar_in[:, :], gsum[:, :, 2], SUBSETS / N, EPS, ALU.mult, ALU.add).then_inc(gvar_part, 1)
                    dve.wait_ge(dev_done, i + 1)
                    nc.vector.tensor_tensor(gdev2[:, :, :], gdev[:, :, :], gdev[:, :, :], ALU.mult).then_inc(dev2_ready, 1)
                elif kind == "row":
                    row(i, f)
                elif kind == "gnb":
                    nc.vector.reduce_sum(gvar_of[:, :], SB[:, 0:CC * SUBSETS].rearrange("p (c s) -> p c s", c=CC),
                                         AX.X).then_inc(read["gnb"], 1)
                    dve.wait_ge(read["gnb"], i + 1)
                    dve.wait_ge(gvar_part, i + 1)
                    nc.vector.tensor_tensor(gvar[:, :], gvar_of[:, :], gvar_in[:, :], ALU.add).then_inc(gvar_ready, 1)
                elif kind == "qk":
                    p, isq, hf = f // 4, f % 4 // 2, f % 2
                    hi = Q1 if isq else K1
                    col = V_QKVB + (0 if isq else 2) + p
                    for a in range(2):
                        h = 2 * p + a
                        dve.wait_ge(qk_hi, 2 * (8 * i + f) + a + 1)
                        dst = Q2[own(a), h, px(hf)] if isq else K1[other(a), h, px(hf)]
                        last = nc.vector.scalar_tensor_tensor(
                            out=dst, in0=SB[own(a), :], scalar=vec[own(a), col:col + 1],
                            in1=hi[own(a), h, px(hf)].bitcast(F32), op0=ALU.add, op1=ALU.subtract)
                    last.then_inc(read["qk"], 1)
                elif kind == "proj":
                    oc, hf = f // NH, f % NH
                    dve.wait_ge(x2_loaded, 16 * i + 16)
                    nc.vector.scalar_tensor_tensor(out=x2[:, oc, px(hf)], in0=SB[:, :], scalar=pbias[:, oc:oc + 1],
                                                   in1=x2[:, oc, px(hf)], op0=ALU.add, op1=ALU.add,
                                                   accum_out=pool4[:, oc, hf:hf + 1]).then_inc(read["proj"], 1)
                    if f == 3:
                        dve.wait_ge(read["proj"], 4 * i + 4)
                        nc.vector.tensor_tensor(pool2[:, :], pool4[:, :, 0], pool4[:, :, 1], ALU.add).then_inc(pool_done, 1)
                        dve.wait_ge(pool_done, 2 * i + 1)
                        for c in range(CC):
                            last = nc.vector.tensor_scalar(poolb[:, c, :], ones[:, :], pool2[:, c:c + 1], None, ALU.mult)
                        last.then_inc(pool_done, 1)
                elif kind == "router":
                    nc.vector.scalar_tensor_tensor(out=logit[:, :], in0=SB[:, 0:E], scalar=1.0 / N, in1=rbias[:, :],
                                                   op0=ALU.mult, op1=ALU.add).then_inc(read["router"], 1)
                elif kind == "conv3":
                    oc, hf = f // NH, f % NH
                    if f >= YBUF:
                        wait(dve, y_stored[f - YBUF], 16 * i + 16)
                    else:
                        wait(dve, y_stored[f + YBUF if f + YBUF < 4 else f], 16 * i)
                    nc.vector.scalar_tensor_tensor(out=y[:, f % YBUF, :], in0=SB[:, :], scalar=bn_s[:, 2 + oc:3 + oc],
                                                   in1=x2[:, oc, px(hf)], op0=ALU.mult, op1=ALU.add).then_inc(read["conv3"], 1)

            def reciprocal(i, f, part):
                cols = slice(part * HALF // 2, (part + 1) * HALF // 2)
                dve.wait_ge(read["z"], 4 * i + f + 1)
                nc.vector.reciprocal(rz[:, f % 2, cols], rz[:, f % 2, cols]).then_inc(rz_ready, 1)

            def normalise_o(i, f):
                reciprocal(i, f, 1)
                dve.wait_ge(rz_ready, 2 * (4 * i + f) + 2)
                dve.wait_ge(o_saved, BLOCKS * i + f + 1)
                wait(dve, filled["proj"], 4 * i)
                nc.vector.tensor_tensor(o[:, f // NH, px(f % NH)], o_raw[:, f % 2, :], rz[:, f % 2, :],
                                        ALU.mult).then_inc(o_norm, 1)

            def gates(i):
                dve.wait_ge(rexp_ready, i + 1)
                nc.vector.tensor_scalar(rden[:, :], rexp[:, :], 1.0, None, ALU.add).then_inc(rw_chain, 1)
                dve.wait_ge(rw_chain, 2 * i + 1)
                nc.vector.reciprocal(rw[:, :], rden[:, :]).then_inc(rw_chain, 1)
                dve.wait_ge(rw_chain, 2 * i + 2)

            def mix_experts(i, e0, e1):
                for e in range(e0, e1):
                    if e == 0:
                        gates(i)
                        wait(dve, filled["conv3"], 4 * i)
                        nc.vector.tensor_scalar(mix[:, :], ex[:, 0, :], rw[:, 0:1], None, ALU.mult).then_inc(mix_chain, 1)
                    else:
                        dve.wait_ge(mix_chain, E * i + e)
                        nc.vector.scalar_tensor_tensor(out=mix[:, :], in0=ex[:, e, :], scalar=rw[:, e:e + 1], in1=mix[:, :],
                                                       op0=ALU.mult, op1=ALU.add).then_inc(mix_chain, 1)
                    if e == E - 1:
                        dve.wait_ge(mix_chain, E * i + E)
                        for hf in range(NH):
                            last = nc.vector.tensor_copy(mix3[own(hf), hf, :], mix[own(hf), M1 + M2:MIX])
                        last.then_inc(mix_ready, 1)

            dve.wait_ge(const_loaded, 16 * LOADS)
            nc.vector.tensor_scalar(bn_var[:, :], vec[:, V_V:V_V + 4], EPS, None, ALU.add).then_inc(dve_set, 1)
            nc.vector.tensor_copy(w_hi[:, :, :], w_stage).then_inc(dve_set, 1)
            dve.wait_ge(dve_set, 2)
            nc.vector.tensor_tensor(w_lo[:, :, :], w_stage, w_hi[:, :, :].bitcast(F32), ALU.subtract).then_inc(dve_set, 1)
            dve.wait_ge(bn_pow, 1)
            nc.vector.tensor_tensor(bn_s[:, :], bn_rs[:, :], vec[:, V_G:V_G + 4], ALU.mult).then_inc(dve_set, 1)
            dve.wait_ge(dve_set, 4)
            nc.vector.tensor_tensor(bn_ms[:, :], bn_s[:, :], vec[:, V_M:V_M + 4], ALU.mult).then_inc(dve_set, 1)
            dve.wait_ge(dve_set, 5)
            nc.vector.tensor_tensor(bn_c[:, :], vec[:, V_B:V_B + 4], bn_ms[:, :], ALU.subtract).then_inc(dve_set, 1)
            dve.wait_ge(bias_filled, 1)
            nc.vector.tensor_tensor(pbias[:, :], MS[:, 0, 0:CC], vec[:, V_PROJB:V_PROJB + CC], ALU.add).then_inc(dve_set, 1)
            for c in range(CC):
                stats(0, c)
            for kind, i, f in PROLOGUE:
                job(kind, i, f)
                if kind == "gnb":
                    affine(0)
                    split_x(0, 0)
                    split_x(0, 1)
            for at in PROLOGUE_FILLS[:16]:
                max_reduce(*at)
            job("row", 0, 0)
            for at in PROLOGUE_FILLS[16:]:
                max_reduce(*at)

            def section(i, first, last):
                mixed = 0
                for s in range(STEPS):
                    fills = fills_at(i, s, last)
                    jobs = jobs_of(s, first, last)
                    slow = [j for j in jobs if j[0] == "qk" or is_second(s, j)]
                    for at in fills[0:1]:
                        max_reduce(*at)
                    for kind, di, f in jobs:
                        if (kind, di, f) not in slow:
                            job(kind, i + di, f)
                    for at in fills[1:2]:
                        max_reduce(*at)
                    for kind, di, f in slow:
                        job(kind, i + di, f)
                    for at in fills[2:]:
                        max_reduce(*at)
                    if s in NORMALISE and not (first and NORMALISE[s][0] < 0):
                        di, f = NORMALISE[s]
                        reciprocal(i + di, f, 0)
                    if s - 1 in NORMALISE and not (first and NORMALISE[s - 1][0] < 0):
                        di, f = NORMALISE[s - 1]
                        normalise_o(i + di, f)
                    if s in STATS_STEPS and not last:
                        stats(i + 1, STATS_STEPS.index(s))
                    if s == AFFINE_STEP and not last:
                        affine(i + 1)
                    if s in SPLIT_STEPS and not last:
                        split_x(i + 1, SPLIT_STEPS.index(s))
                    if s in MIX_STEPS and not first:
                        mix_experts(i - 1, mixed, mixed + MIX_STEPS[s])
                        mixed += MIX_STEPS[s]

            sections(dve, section)
            for kind, _, f in EPILOGUE:
                job(kind, B - 1, f)
                if kind == "z":
                    reciprocal(B - 1, f, 0)
                    normalise_o(B - 1, f)
                if kind == "router":
                    mix_experts(B - 1, 0, E)


_ORDER = ["x", "vecs", "router_b", "wqkv", "wproj", "wrouter", "experts", "neg_eye", "group_avg"]


def _chunks(v):
    return np.asarray(v).reshape(-1, P).T


def kernel(**inputs):
    import concourse.bacc as _bacc
    from concourse.bass_utils import run_bass_kernel_spmd as _run

    a = {k: np.asarray(v) for k, v in inputs.items()}
    c1 = {k[len("L1_conv_"):]: v for k, v in a.items() if k.startswith("L1_conv_")}

    def layers(k):
        return np.concatenate([np.tile(c1[k + "1"], 2)[:, None], np.tile(c1[k + "2"], 2)[:, None], _chunks(c1[k + "3"])], axis=1)

    vecs = np.concatenate([_chunks(a["L0_conv_gn_w"]), _chunks(a["L0_conv_gn_b"]), _chunks(a["L0_conv_qkv_b"]),
                           _chunks(a["L0_conv_proj_b"]), layers("g"), layers("b"), layers("m"), layers("v")], axis=1)

    def stationary(w):
        return w.T.reshape(CC, P, -1).transpose(1, 0, 2)

    e1 = c1["w1"][:, :, :, 0, 0].transpose(2, 0, 1).reshape(CC, P, E, WID).transpose(1, 2, 0, 3).reshape(P, E, M1)
    w2 = c1["w2"].transpose(4, 2, 0, 3, 1)
    low = np.concatenate([w2[0], w2[2]], axis=2)
    high = np.concatenate([w2[1], np.zeros_like(w2[1])], axis=2)
    e2 = np.concatenate([low, high], axis=0).reshape(P, E, M2)
    w3 = c1["w3"][:, :, :, 0, 0].transpose(2, 0, 1)
    e3 = np.concatenate([w3, w3], axis=0)
    arrays = {
        "x": a["x"].reshape(B, CC, P, N),
        "vecs": vecs,
        "router_b": np.broadcast_to(c1["router_b"], (P, E)),
        "wqkv": stationary(a["L0_conv_qkv_w"]),
        "wproj": stationary(a["L0_conv_proj_w"]),
        "wrouter": stationary(c1["router_w"]),
        "experts": np.concatenate([e1, e2, e3], axis=2),
        "neg_eye": -np.eye(P, dtype=np.float32),
        "group_avg": np.kron(np.eye(P // GROUP, dtype=np.float32), np.full((GROUP, GROUP), 1 / (GROUP * SUBSETS), np.float32)),
    }
    nc = _bacc.Bacc("TRN2", target_bir_lowering=False, num_devices=1)
    data, args = {}, []
    for name in _ORDER:
        v = np.ascontiguousarray(arrays[name])
        data[f"in_{name}_dram"] = v
        ap = nc.dram_tensor(f"in_{name}_dram", v.shape, mybir.dt.from_np(v.dtype), kind="ExternalInput").ap()
        args.append(ap.rearrange("b c p n -> b p c n") if name == "x" else ap)
    res = nc.dram_tensor("out_0_dram", (B, CC, P, N), F32, kind="ExternalOutput").ap()
    build(nc, *args, res.rearrange("b c p n -> b p c n"))
    r = _run(nc, [data], core_ids=[0])
    return r.results[0]["out_0_dram"].reshape(B, C, H, W)
```

```python
from contextlib import ExitStack

import numpy as np

import concourse.bass as bass
from concourse import mybir

F32 = mybir.dt.float32
F32R = mybir.dt.float32r
ALU = mybir.AluOpType
ACT = mybir.ActivationFunctionType
AX = mybir.AxisListType

B, C, H, W = 16, 256, 32, 32
N = H * W
P = 128
CC = C // P
HEADS, D = 4, 64
PAIRS = HEADS // 2
HALF = 512
NH = N // HALF
KT = N // P
QT = HALF // P
BLOCKS = PAIRS * NH
STEPS = BLOCKS * KT
GROUP = 8
SUBSETS = 2 * NH
E = 8
WID = 64
EPS = 1e-5
PW = W + 2
PAD = (H + 2) * PW
TAPS = 6
M1, M2, M3 = CC * WID, TAPS * WID, C
MIX = M1 + M2 + M3
YBUF = 3
PBUF = 3

V_GNW, V_GNB, V_QKVB, V_PROJB, V_G, V_B, V_M, V_V = 0, 2, 4, 10, 12, 16, 20, 24
VECS = 28

SIDE = {
    0: [("z", -1, 3)], 1: [("qk", 0, 5), ("proj", -1, 0)], 2: [("qk", 0, 6), ("qk", 0, 7)], 3: [("proj", -1, 1)],
    4: [None, ("row", 0, 1)], 5: [("proj", -1, 2)], 7: [("proj", -1, 3), ("gna", 1, 0)],
    8: [("router", -1, 0), ("gnb", 1, 0)], 12: [None, ("row", 0, 2)], 15: [None, ("z", 0, 0)], 16: [("qk", 1, 0)],
    17: [("qk", 1, 1)], 18: [("qk", 1, 2)], 19: [("qk", 1, 3)], 20: [("conv1", -1, 0)], 21: [("row", 0, 3)],
    22: [("v", 1, 0), ("v", 1, 1)], 23: [("conv2a", -1, 0)], 24: [("conv2", -1, 0), ("z", 0, 1)],
    25: [None, ("conv3", -1, 0)], 26: [None, ("z", 0, 2)], 27: [None, ("conv3", -1, 1)], 28: [None, ("v", 1, 2)],
    29: [("conv3", -1, 2), ("row", 1, 0)], 30: [("v", 1, 3), ("conv3", -1, 3)], 31: [("qk", 1, 4)],
}
NORMALISE = {0: (-1, 3), 21: (0, 0), 26: (0, 1), 29: (0, 2)}
PROLOGUE = [("gna", 0, 0), ("gnb", 0, 0)] + [("qk", 0, f) for f in range(4)] + [("v", 0, f) for f in range(4)] + [("qk", 0, 4), ("bias", 0, 0)]
EPILOGUE = ([("z", 0, 3)] + [("proj", 0, f) for f in range(4)] + [("router", 0, 0), ("conv1", 0, 0),
            ("conv2a", 0, 0), ("conv2", 0, 0)] + [("conv3", 0, f) for f in range(4)])
FILLS_AHEAD = 6
FILLS = [3, 3, 2, 2, 0, 3, 3, 2, 3, 1, 2, 3, 1, 1, 1, 1, 2, 2, 3, 2, 2, 0, 3, 2, 3, 3, 1, 3, 1, 2, 3, 1]
STATS_STEPS, AFFINE_STEP, NORM_STEPS, SPLIT_STEPS = (3, 6), 9, (11, 14), (13, 14)
MIX_STEPS = {8: 1, 10: 1, 12: 2, 14: 1, 16: 1, 17: 1, 18: 1}


def build(nc, x, vecs, router_b, wqkv, wproj, wrouter, experts, neg_eye, group_avg, out):
    ctx = ExitStack()
    with ctx:
        def sb(name, shape, dt=F32):
            return ctx.enter_context(nc.sbuf_tensor(name, shape, dt))

        def pb(name, shape):
            return ctx.enter_context(nc.psum_tensor(name, shape, F32))

        def sem(name):
            return ctx.enter_context(nc.semaphore(name))

        vec = sb("vec", [P, VECS])
        rbias = sb("rbias", [P, E])
        w_hi = sb("w_hi", [P, CC, 3 * C], F32R)
        w_lo = sb("w_lo", [P, CC, 3 * C], F32R)
        wp = sb("wp", [P, CC, C])
        wr = sb("wr", [P, CC, E])
        ex = sb("ex", [P, E, MIX])
        negeye = sb("negeye", [P, P])
        gavg = sb("gavg", [P, P])
        ones = sb("ones", [P, P])
        neghalf = sb("neghalf", [P, 4])
        pbias = sb("pbias", [P, CC])
        bn_var = sb("bn_var", [P, 4])
        bn_rs = sb("bn_rs", [P, 4])
        bn_s = sb("bn_s", [P, 4])
        bn_ms = sb("bn_ms", [P, 4])
        bn_c = sb("bn_c", [P, 4])
        xin = sb("xin", [P, CC, N])
        x_hi = sb("x_hi", [P, CC, N], F32R)
        x_lo = sb("x_lo", [P, CC, N], F32R)
        Q1 = sb("Q1", [P, HEADS, N], F32R)
        Q2 = sb("Q2", [P, HEADS, N], F32R)
        K1 = sb("K1", [P, HEADS, N], F32R)
        K2 = sb("K2", [P, HEADS, N], F32R)
        V = sb("V", [P, PAIRS, KT, P])
        v_next = sb("v_next", [P, KT, P])
        prob = sb("prob", [P, PBUF, 2, HALF])
        w_stage = prob[:, :, :, :].rearrange("p b a n -> p (b a n)")[:, 0:CC * 3 * C].rearrange("p (c n) -> p c n", c=CC)
        psum_p = sb("psum_p", [P, 2, 2, HALF])
        qk_raw = sb("qk_raw", [P, 2, HALF])
        o_raw = sb("o_raw", [P, 2, HALF])
        rz = sb("rz", [P, 2, HALF])
        o = sb("o", [P, CC, N])
        x2 = sb("x2", [P, CC, N])
        hpad = sb("hpad", [P, PAD + 2])
        h2 = sb("h2", [P, HALF])
        y = sb("y", [P, YBUF, HALF])
        mix = sb("mix", [P, MIX])
        mix3 = sb("mix3", [P, NH, C])
        mx = sb("mx", [P, 2, 2 * QT, NH])
        mx1 = sb("mx1", [P, 2 * QT])
        mrow = sb("mrow", [2 * QT, P], F32R)
        bst = sb("bst", [P, CC, SUBSETS, 3])
        gsum = sb("gsum", [P, CC, 3])
        gdev = sb("gdev", [P, CC, SUBSETS])
        gdev2 = sb("gdev2", [P, CC, SUBSETS])
        gvar_in = sb("gvar_in", [P, CC])
        gvar_of = sb("gvar_of", [P, CC])
        gvar = sb("gvar", [P, CC])
        grs = sb("grs", [P, CC])
        gsc = sb("gsc", [P, CC])
        gms = sb("gms", [P, CC])
        gbi = sb("gbi", [P, CC])
        pool4 = sb("pool4", [P, CC, NH])
        pool2 = sb("pool2", [P, CC])
        poolb = sb("poolb", [P, CC, P])
        logit = sb("logit", [P, E])
        rexp = sb("rexp", [P, E])
        rden = sb("rden", [P, E])
        rw = sb("rw", [P, E])

        S = pb("S", [P, 2, 2, HALF])
        MS = pb("MS", [P, 2, HALF])
        PV = pb("PV", [P, HALF])
        SB = pb("SB", [P, HALF])

        norm_loaded = sem("norm_loaded")
        wqkv_loaded = sem("wqkv_loaded")
        rest_loaded = sem("rest_loaded")
        consts_set = sem("consts_set")
        dve_set = sem("dve_set")
        w_hi_ready = sem("w_hi_ready")
        bn_pow = sem("bn_pow")
        xin_loaded = sem("xin_loaded")
        x2_loaded = sem("x2_loaded")
        v1_loaded = sem("v1_loaded")
        rows_loaded = sem("rows_loaded")
        dup_loaded = [sem(f"dup{n}_loaded") for n in range(PAIRS)]
        y_stored = [sem(f"y{f}_stored") for f in range(4)]
        s_done = sem("s_done")
        exp_done = sem("exp_done")
        pv_done = sem("pv_done")
        add_done = sem("add_done")
        o_saved = sem("o_saved")
        o_norm = sem("o_norm")
        rz_ready = sem("rz_ready")
        max_filled = sem("max_filled")
        max_read = sem("max_read")
        max_ready = sem("max_ready")
        h_saved = sem("h_saved")
        filled = {k: sem(k + "_filled") for k in ("qk", "v", "z", "proj", "gna", "gnb", "router", "conv1", "conv2", "conv3", "row", "bias")}
        read = {k: sem(k + "_read") for k in ("qk", "v", "z", "proj", "gna", "gnb", "router", "conv1", "conv2", "conv3", "row", "bias")}
        per_image = {"bias": 1, "row": BLOCKS, "qk": 8, "v": 4, "z": 4, "proj": 4, "gna": 1, "gnb": 1, "router": 1, "conv1": 1, "conv2": 1, "conv3": 4}
        qk_hi = sem("qk_hi")
        qk_lo = sem("qk_lo")
        stats_ready = sem("stats_ready")
        gvar_part = sem("gvar_part")
        gvar_ready = sem("gvar_ready")
        dev_done = sem("dev_done")
        dev2_ready = sem("dev2_ready")
        rs_ready = sem("rs_ready")
        aff = sem("aff")
        xn_ready = sem("xn_ready")
        xsplit_ready = sem("xsplit_ready")
        pool_done = sem("pool_done")
        rexp_ready = sem("rexp_ready")
        rw_chain = sem("rw_chain")
        mix_chain = sem("mix_chain")
        mix_ready = sem("mix_ready")
        mix_rest_ready = sem("mix_rest_ready")
        y_ready = sem("y_ready")

        DVE_SET, CONSTS_SET = 5, 4 + 3 * HEADS

        BANKS = [SB[:, :], PV[:, :]] + [S[:, t, a, :] for t in range(2) for a in range(2)]

        BEFORE_PAIRS, JOB_AFTER_PAIR = 8, (2, 3, 5, 7)
        PAIR_BANKS = [MS[:, :, :], S[:, 0, :, :], S[:, 1, :, :]]

        def in_turn(jobs, all_banks=len(EPILOGUE)):
            turns = []
            for kind, _, f in jobs:
                if kind == "conv2":
                    turns.append((kind, f, turns[-1][2], None))
                else:
                    n = sum(t[0] != "conv2" for t in turns)
                    bank = BANKS[n % (len(BANKS) if n < all_banks else 2)]
                    users = [t for t in turns if t[2] is bank and t[0] != "conv2a"]
                    turns.append((kind, f, bank, users[-1][:2] if users else None))
            return turns

        block = ctx.enter_context(nc.Block())

        def wait(eng, s, value):
            if not isinstance(value, int) or value > 0:
                eng.wait_ge(s, value)

        def adds_reading(g_image, s):
            return g_image * (STEPS - BLOCKS) + (s // KT) * (KT - 1) + max(1, s % KT)

        def done(kind, i, f):
            return per_image[kind] * i + f + 1

        def jobs_of(s, first, last):
            gone = {-1} if first else set()
            gone |= {1} if last else set()
            return [j for j in SIDE.get(s, []) if j and j[1] not in gone]

        def sections(eng, section):
            section(0, True, False)
            section(1, False, False)
            with eng.Fori(2, B - 1) as i:
                section(i, False, False)
            section(B - 1, False, True)

        def is_second(s, job):
            return SIDE[s].index(job) == 1

        def fills_at(i, s, last):
            first_fill = 16 + FILLS_AHEAD + sum(FILLS[:s])
            fills = [divmod(n, 16) for n in range(first_fill, first_fill + FILLS[s])]
            return [(i + b // BLOCKS, b % BLOCKS, m) for b, m in fills if not (last and b >= BLOCKS)]

        FIRST_PAIRS = (16 + FILLS_AHEAD) // 2

        def own(a):
            return slice(64 * a, 64 * a + 64)

        def other(a):
            return slice(64 - 64 * a, 128 - 64 * a)

        def px(hf):
            return slice(hf * HALF, hf * HALF + HALF)

        @block.sync
        def _(sp):
            def load_xin(i):
                if not isinstance(i, int) or i > 0:
                    wait(sp, xsplit_ready, 2 * i)
                sp.dma_start(xin[:, :, :], x[i]).then_inc(xin_loaded, 16)

            def load_x2(i):
                wait(sp, read["conv3"], 4 * i)
                sp.dma_start(x2[:, :, :], x[i]).then_inc(x2_loaded, 16)

            def load_v1(i):
                sp.wait_ge(pv_done, STEPS * i + 1)
                sp.dma_start(V[:, 1, :, :], v_next[:, :, :]).then_inc(v1_loaded, 16)

            def dup(i, f):
                p, kind, hf = f // 4, f % 4 // 2, f % 2
                for a in range(2):
                    sp.wait_ge(qk_hi, 2 * (8 * i + f) + a + 1)
                    h = 2 * p + a
                    if kind:
                        src, dst = Q1[own(a), h, px(hf)], Q1[other(a), h, px(hf)]
                    else:
                        src, dst = K1[own(a), h, px(hf)], K2[own(a), h, px(hf)]
                    sp.dma_start(dst.bitcast(F32), src.bitcast(F32)).then_inc(dup_loaded[p], 16)

            def rows(i, b):
                p, hf = b // NH, b % NH
                sp.wait_ge(read["row"], BLOCKS * i + b + 1)
                for a in range(2):
                    r = 64 - 64 * a
                    sp.dma_start(Q2[r:r + 1, 2 * p + a, px(hf)].bitcast(F32),
                                 mrow[QT * a:QT * a + QT, :].bitcast(F32)).then_inc(rows_loaded, 16)

            def shift_h(i):
                sp.wait_ge(read["conv1"], i + 1)
                sp.dma_start(hpad[64:128, 0:PAD], hpad[0:64, 1:PAD + 1]).then_inc(h_saved, 16)

            def store(i, f):
                oc, hf = f // NH, f % NH
                sp.wait_ge(y_ready, 4 * i + f + 1)
                sp.dma_start(out[i, :, oc, px(hf)], y[:, f % YBUF, :]).then_inc(y_stored[f], 16)

            def section(i, first, last):
                load_v1(i)
                for s in range(STEPS):
                    for kind, di, f in jobs_of(s, first, last):
                        if kind == "qk":
                            dup(i + di, f)
                        if kind == "row":
                            rows(i + di, f)
                        if kind == "conv1":
                            shift_h(i + di)
                        if kind == "conv3":
                            store(i + di, f)
                    if s == STEPS - 1:
                        load_x2(i)
                    if s == 0 and not last:
                        load_xin(i + 1)

            load_xin(0)
            sp.dma_start(vec[:, :], vecs).then_inc(norm_loaded, 16)
            sp.dma_start(gavg[:, :], group_avg).then_inc(norm_loaded, 16)
            sp.dma_start(w_stage, wqkv).then_inc(wqkv_loaded, 16)
            sp.dma_start(negeye[:, :], neg_eye).then_inc(rest_loaded, 16)
            sp.dma_start(wp[:, :, :], wproj).then_inc(rest_loaded, 16)
            sp.dma_start(wr[:, :, :], wrouter).then_inc(rest_loaded, 16)
            sp.dma_start(rbias[:, :], router_b).then_inc(rest_loaded, 16)
            sp.dma_start(ex[:, :, :], experts).then_inc(rest_loaded, 16)
            for f in range(5):
                dup(0, f)
            sp.wait_ge(consts_set, CONSTS_SET)
            rows(0, 0)
            sections(sp, section)
            shift_h(B - 1)
            for f in range(4):
                store(B - 1, f)
            for f in range(4):
                sp.wait_ge(y_stored[f], 16 * B)

        @block.gpsimd
        def _(pool):
            def rstd(i):
                pool.wait_ge(gvar_ready, i + 1)
                nc.gpsimd.tensor_tensor(grs[:, :], gvar[:, :], neghalf[:, 0:CC], ALU.pow).then_inc(rs_ready, 1)

            nc.gpsimd.memset(neghalf[:, :], -0.5).then_inc(consts_set, 1)
            pool.wait_ge(consts_set, 1)
            pool.wait_ge(dve_set, 1)
            nc.gpsimd.tensor_tensor(bn_rs[:, :], bn_var[:, :], neghalf[:, :], ALU.pow).then_inc(bn_pow, 1)
            rstd(0)
            count = 1
            fills = [(ones[:, :], 1.0), (hpad[:, :], 0.0), (mix3[:, :, :], 0.0)]
            for h in range(HEADS):
                r = 64 - 64 * (h % 2)
                fills += [(t[other(h % 2), h, :].bitcast(F32), 0.0) for t in (Q2, K2)]
                fills += [(K2[r:r + 1, h, :].bitcast(F32), 1.0)]
            for dst, value in fills:
                nc.gpsimd.memset(dst, value).then_inc(consts_set, 1)
                count += 1
                pool.wait_ge(consts_set, count)

            def section(i, first, last):
                for s in range(STEPS):
                    b, j = s // KT, s % KT
                    acc = psum_p[:, b % 2, :, :]
                    if j == 1:
                        wait(pool, filled["z"], BLOCKS * i + b - 1)
                    if j > 0:
                        pool.wait_ge(exp_done, STEPS * i + s + 1)
                        if j > 1:
                            pool.wait_ge(add_done, adds_reading(i, s) - 1)
                        first_in = prob[:, (s - 1) % PBUF, :, :] if j == 1 else acc
                        nc.gpsimd.tensor_tensor(acc, first_in, prob[:, s % PBUF, :, :], ALU.add).then_inc(add_done, 1)
                    if s == AFFINE_STEP - 1 and not last:
                        rstd(i + 1)

            sections(pool, section)

        @block.tensor
        def _(pe):
            def split_mm(dst, wl, xl, pairs):
                k = 0
                for c in range(CC):
                    for w, m in pairs:
                        last = nc.tensor.matmul(dst, wl(w, c), xl(m, c), start=(k == 0), stop=(k == 3 * CC - 1))
                        k += 1
                return last

            def job(kind, i, f, before, bank=SB[:, :], at_end=False):
                for k, bi, bf in before:
                    pe.wait_ge(read[k], done(k, bi, bf))
                if kind == "gna":
                    pe.wait_ge(stats_ready, CC * i + CC)
                    last = nc.tensor.matmul(bank[:, 0:CC * SUBSETS * 3], gavg[:, :], bst[:, :, :, :].rearrange("p c s k -> p (c s k)"), start=True, stop=True)
                elif kind == "gnb":
                    pe.wait_ge(dev2_ready, i + 1)
                    last = nc.tensor.matmul(bank[:, 0:CC * SUBSETS], gavg[:, :], gdev2[:, :, :].rearrange("p c s -> p (c s)"), start=True, stop=True)
                elif kind == "qk":
                    p, isq, hf = f // 4, f % 4 // 2, f % 2
                    if f == 0:
                        pe.wait_ge(xsplit_ready, 2 * i + 2)
                        if isinstance(i, int) and i == 0:
                            pe.wait_ge(dve_set, 2)
                    col = (0 if isq else C) + p * P
                    last = split_mm(bank, lambda w, c: w[:, c, col:col + P], lambda m, c: m[:, c, px(hf)],
                                    ((w_hi, x_hi), (w_hi, x_lo), (w_lo, x_hi)))
                elif kind == "v":
                    for t in (0, 1):
                        kt = 2 * f + t
                        last = split_mm(bank[:, t * C:t * C + C], lambda w, c: w[:, c, kt * P:kt * P + P],
                                        lambda m, c: m[:, c, 2 * C:3 * C], ((x_hi, w_hi), (x_lo, w_hi), (x_hi, w_lo)))
                elif kind == "z":
                    pe.wait_ge(add_done, adds_reading(i, KT * f + KT - 1))
                    for a in range(2):
                        last = nc.tensor.matmul(bank[own(a), :], ones[:, 0:D], psum_p[:, f % 2, a, :], start=True, stop=True)
                elif kind == "proj":
                    hf, oc = f // CC, f % CC
                    if oc == 0:
                        pe.wait_ge(o_norm, BLOCKS * i + BLOCKS - 1 + hf)
                    for c in range(CC):
                        last = nc.tensor.matmul(bank, wp[:, c, oc * P:oc * P + P], o[:, c, px(hf)],
                                                start=(c == 0), stop=(c == CC - 1))
                elif kind == "row":
                    pe.wait_ge(max_ready, BLOCKS * i + f + 1)
                    last = nc.tensor.matmul(bank[0:2 * QT, 0:P], mx1[:, :], negeye[:, :], start=True, stop=True)
                elif kind == "bias":
                    pe.wait_ge(rest_loaded, 16 * 5)
                    for oc in range(CC):
                        for c in range(CC):
                            last = nc.tensor.matmul(bank[:, oc:oc + 1], wp[:, c, oc * P:oc * P + P], vec[:, V_QKVB + 4 + c:V_QKVB + 5 + c],
                                                    start=(c == 0), stop=(c == CC - 1))
                elif kind == "router":
                    pe.wait_ge(pool_done, 2 * i + 2)
                    for c in range(CC):
                        last = nc.tensor.matmul(bank[:, 0:E], poolb[:, c, :], wr[:, c, :], start=(c == 0), stop=(c == CC - 1))
                elif kind == "conv1":
                    pe.wait_ge(mix_ready, i + 1)
                    for c in range(CC):
                        for hf in range(NH):
                            last = nc.tensor.matmul(bank[own(hf), :], mix[:, c * WID:c * WID + WID], x2[:, c, px(hf)],
                                                    start=(c == 0), stop=(c == CC - 1))
                elif kind in ("conv2a", "conv2"):
                    if kind == "conv2a":
                        pe.wait_ge(h_saved, 16 * i + 16)
                        if at_end:
                            pe.wait_ge(mix_rest_ready, 1)
                    rows_hf = H // NH
                    for tap in (range(3) if kind == "conv2a" else range(3, 6)):
                        dy, dx = tap % 3, 2 * (tap // 3)
                        for hf in range(NH):
                            at = (dy + hf * rows_hf) * PW + dx
                            src = hpad[:, at:at + rows_hf * PW].rearrange("p (r w) -> p r w", w=PW)[:, :, 0:W]
                            last = nc.tensor.matmul(bank[own(hf), :], mix[:, M1 + tap * WID:M1 + tap * WID + WID], src,
                                                    start=(tap == 0), stop=(tap == TAPS - 1))
                elif kind == "conv3":
                    oc, hf = f // NH, f % NH
                    if f == 0:
                        pe.wait_ge(read["conv2"], i + 1)
                        if at_end:
                            pe.wait_ge(mix_rest_ready, 2)
                    last = nc.tensor.matmul(bank, mix3[:, hf, oc * P:oc * P + P], h2[:, :], start=True, stop=True)
                if kind != "conv2a":
                    last.then_inc(filled[kind], 1)

            def max_fill(i, b, m):
                p, hf, a, t, nh = b // NH, b % NH, m // (2 * QT), m // 2 % QT, m % 2
                h = 2 * p + a
                if m == 0:
                    pe.wait_ge(qk_lo, 8 * i + 4 * p + 4)
                    pe.wait_ge(dup_loaded[p], 32 * 4 * (i + 1))
                wait(pe, max_read, 64 * i + 16 * b + m - 1)
                q0 = hf * HALF + t * P
                nc.tensor.matmul(MS[:, m % 2, :], Q1[:, h, q0:q0 + P], K1[:, h, px(nh)],
                                 start=True, stop=True).then_inc(max_filled, 1)

            def max_fill_pair(n, b, m):
                if n >= 3:
                    pe.wait_ge(max_read, 2 * (n - 2))
                h, q0 = m // (2 * QT), b * HALF + m // 2 % QT * P
                for nh in range(NH):
                    nc.tensor.matmul(PAIR_BANKS[n % 3][:, nh, :], Q1[:, h, q0:q0 + P], K1[:, h, px(nh)],
                                     start=True, stop=True).then_inc(max_filled, 1)

            def scores(i, s):
                b, kt = s // KT, s % KT
                p, hf = b // NH, b % NH
                wait(pe, exp_done, STEPS * i + s - 1)
                for a in range(2):
                    h = 2 * p + a
                    nc.tensor.matmul(S[:, s % 2, a, :], K1[:, h, kt * P:kt * P + P], Q1[:, h, px(hf)], start=True, stop=False)
                    if kt == 0 and a == 0:
                        pe.wait_ge(rows_loaded, 32 * (BLOCKS * i + b + 1))
                    last = nc.tensor.matmul(S[:, s % 2, a, :], K2[:, h, kt * P:kt * P + P], Q2[:, h, px(hf)], start=False, stop=True)
                last.then_inc(s_done, 1)

            def pv(i, s):
                b, kt = s // KT, s % KT
                if s == 0:
                    pe.wait_ge(read["v"], 4 * i + 4)
                if s == KT * NH:
                    pe.wait_ge(v1_loaded, 16 * i + 16)
                if kt == 0:
                    wait(pe, o_saved, BLOCKS * i + b)
                pe.wait_ge(exp_done, STEPS * i + s + 1)
                for a in range(2):
                    last = nc.tensor.matmul(PV[own(a), :], V[:, b // NH, kt, a * D:a * D + D], prob[:, s % PBUF, a, :],
                                            start=(kt == 0), stop=(kt == KT - 1))
                last.then_inc(pv_done, 1)

            pe.wait_ge(norm_loaded, 32)
            turns = in_turn(PROLOGUE, len(BANKS))
            for kind, f, bank, last_user in turns[:BEFORE_PAIRS]:
                job(kind, 0, f, [(last_user[0], 0, last_user[1])] if last_user else [], bank)
            pe.wait_ge(qk_lo, 4)
            pe.wait_ge(dup_loaded[0], 32 * 4)
            for n in range(FIRST_PAIRS):
                max_fill_pair(n, n // 8, 2 * n % 16)
                if n in JOB_AFTER_PAIR:
                    kind, f, bank, last_user = turns[BEFORE_PAIRS + JOB_AFTER_PAIR.index(n)]
                    job(kind, 0, f, [(last_user[0], 0, last_user[1])], bank)
                if n == 9:
                    pe.wait_ge(read["qk"], 5)
                    job("row", 0, 0, [])
            pe.wait_ge(max_read, 2 * FIRST_PAIRS)
            pe.wait_ge(consts_set, CONSTS_SET)
            scores(0, 0)

            last_job = SIDE[max(SIDE)][-1]

            def section(i, first, last):
                held = [("row", 0, 0)] if first else [(last_job[0], i - 1 + last_job[1], last_job[2])]
                for s in range(STEPS):
                    fills = fills_at(i, s, last)
                    jobs = jobs_of(s, first, last)
                    if s < STEPS - 1:
                        scores(i, s + 1)
                    elif not last:
                        scores(i + 1, 0)
                    for at in fills[0:1]:
                        max_fill(*at)
                    for second in (False, True):
                        for j in jobs:
                            if is_second(s, j) == second:
                                kind, di, f = j
                                job(kind, i + di, f, [] if kind == "conv2" else held)
                                held = [(kind, i + di, f)]
                        if not second:
                            for at in fills[1:2]:
                                max_fill(*at)
                            pv(i, s)
                            for at in fills[2:]:
                                max_fill(*at)

            sections(pe, section)
            kind, di, f = [j for s in sorted(SIDE) for j in jobs_of(s, False, True)][-1]
            pe.wait_ge(read[kind], done(kind, B - 1 + di, f))
            pe.wait_ge(o_saved, BLOCKS * B)
            for kind, f, bank, last_user in in_turn(EPILOGUE):
                job(kind, B - 1, f, [(last_user[0], B - 1, last_user[1])] if last_user else [], bank, at_end=True)

        @block.scalar
        def _(act):
            def exps(i, s):
                before = s - PBUF if s >= PBUF else max(r for r in range(STEPS) if r % PBUF == s % PBUF) - STEPS
                wait(act, pv_done, STEPS * i + before + 1)
                if before >= 0:
                    act.wait_ge(add_done, adds_reading(i, before))
                elif not isinstance(i, int) or i > 0:
                    act.wait_ge(add_done, adds_reading(i - 1, STEPS + before))
                act.wait_ge(s_done, STEPS * i + s + 1)
                nc.scalar.activation(prob[:, s % PBUF, :, :], S[:, s % 2, :, :], ACT.Exp, scale=D ** -0.5).then_inc(exp_done, 1)

            def save_o(i, b):
                act.wait_ge(pv_done, STEPS * i + KT * b + KT)
                wait(act, o_norm, BLOCKS * i + b - 1)
                nc.scalar.activation(o_raw[:, b % 2, :], PV[:, :], ACT.Copy).then_inc(o_saved, 1)

            def job(kind, i, f, bank=SB[:, :]):
                if kind == "qk":
                    p, isq, hf = f // 4, f % 4 // 2, f % 2
                    act.wait_ge(filled["qk"], 8 * i + f + 1)
                    wait(act, qk_lo, 8 * i + f - 1)
                    dst = Q1 if isq else K1
                    col = V_QKVB + (0 if isq else 2) + p
                    nc.scalar.activation(qk_raw[:, f % 2, :], bank, ACT.Identity, bias=vec[:, col:col + 1]).then_inc(read["qk"], 1)
                    act.wait_ge(read["qk"], 8 * i + f + 1)
                    wait(act, s_done, STEPS * (i - 1) + KT * NH * (p + 1))
                    for a in range(2):
                        nc.scalar.activation(dst[own(a), 2 * p + a, px(hf)], qk_raw[own(a), f % 2, :], ACT.Copy).then_inc(qk_hi, 1)
                elif kind == "v":
                    act.wait_ge(filled["v"], 4 * i + f + 1)
                    wait(act, pv_done, STEPS * (i - 1) + KT * NH)
                    wait(act, v1_loaded, 16 * i)
                    src = bank.rearrange("p (t q n) -> p t q n", t=2, q=PAIRS)
                    nc.scalar.activation(V[:, 0, 2 * f:2 * f + 2, :], src[:, :, 0, :], ACT.Copy)
                    nc.scalar.activation(v_next[:, 2 * f:2 * f + 2, :], src[:, :, 1, :], ACT.Copy).then_inc(read["v"], 1)
                elif kind == "z":
                    act.wait_ge(filled["z"], 4 * i + f + 1)
                    wait(act, o_norm, 4 * i + f - 1)
                    nc.scalar.activation(rz[:, f % 2, :], bank, ACT.Copy).then_inc(read["z"], 1)
                elif kind == "router":
                    act.wait_ge(read["router"], i + 1)
                    nc.scalar.activation(rexp[:, :], logit[:, :], ACT.Exp, scale=-1.0).then_inc(rexp_ready, 1)
                elif kind == "conv1":
                    act.wait_ge(filled["conv1"], i + 1)
                    rows_hf = H // NH
                    for hf in range(NH):
                        at = (1 + hf * rows_hf) * PW + 1
                        dst = hpad[0:64, at:at + rows_hf * PW].rearrange("p (r w) -> p r w", w=PW)[:, :, 0:W]
                        src = bank[own(hf), :].rearrange("p (r w) -> p r w", w=W)
                        last = nc.scalar.activation(dst, src, ACT.Relu, bias=bn_c[own(hf), 0:1], scale=bn_s[own(hf), 0:1])
                    last.then_inc(read["conv1"], 1)
                elif kind == "conv2":
                    act.wait_ge(filled["conv2"], i + 1)
                    nc.scalar.activation(h2[:, :], bank, ACT.Relu, bias=bn_c[:, 1:2], scale=bn_s[:, 1:2]).then_inc(read["conv2"], 1)
                elif kind == "conv3":
                    oc = f // NH
                    act.wait_ge(read["conv3"], 4 * i + f + 1)
                    nc.scalar.activation(y[:, f % YBUF, :], y[:, f % YBUF, :], ACT.Relu, bias=bn_c[:, 2 + oc:3 + oc]).then_inc(y_ready, 1)

            def normalise(i, c):
                if c == 0:
                    act.wait_ge(aff, 3 * i + 3)
                    wait(act, filled["qk"], 8 * i)
                nc.scalar.activation(x_hi[:, c, :], xin[:, c, :], ACT.Identity, bias=gbi[:, c:c + 1], scale=gsc[:, c:c + 1])
                nc.scalar.activation(xin[:, c, :], xin[:, c, :], ACT.Identity, bias=gbi[:, c:c + 1],
                                     scale=gsc[:, c:c + 1]).then_inc(xn_ready, 1)

            act.wait_ge(wqkv_loaded, 16)
            nc.scalar.activation(w_hi[:, :, :], w_stage, ACT.Copy).then_inc(w_hi_ready, 1)
            for c in range(CC):
                normalise(0, c)
            for kind, f, bank, _ in in_turn(PROLOGUE, len(BANKS)):
                job(kind, 0, f, bank)
            act.wait_ge(dve_set, DVE_SET)
            act.wait_ge(consts_set, CONSTS_SET)
            exps(0, 0)

            def section(i, first, last):
                for s in range(STEPS):
                    if s % KT == 0:
                        if s:
                            save_o(i, s // KT - 1)
                        elif not first:
                            save_o(i - 1, BLOCKS - 1)
                    if s < STEPS - 1:
                        exps(i, s + 1)
                    elif not last:
                        exps(i + 1, 0)
                    for kind, di, f in jobs_of(s, first, last):
                        job(kind, i + di, f)
                    if s in NORM_STEPS and not last:
                        normalise(i + 1, NORM_STEPS.index(s))

            sections(act, section)
            save_o(B - 1, BLOCKS - 1)
            for kind, f, bank, _ in in_turn(EPILOGUE):
                job(kind, B - 1, f, bank)

        @block.vector
        def _(dve):
            def stats(i, c):
                dve.wait_ge(xin_loaded, 16 * i + 16)
                for hf in range(NH):
                    last = nc.vector.bn_stats(bst[:, c, 2 * hf:2 * hf + 2, :].rearrange("p s k -> p (s k)"), xin[:, c, px(hf)])
                last.then_inc(stats_ready, 1)

            def affine(i):
                dve.wait_ge(rs_ready, i + 1)
                nc.vector.tensor_tensor(gsc[:, :], grs[:, :], vec[:, V_GNW:V_GNW + CC], ALU.mult).then_inc(aff, 1)
                dve.wait_ge(aff, 3 * i + 1)
                nc.vector.tensor_tensor(gms[:, :], gsum[:, :, 1], gsc[:, :], ALU.mult).then_inc(aff, 1)
                dve.wait_ge(aff, 3 * i + 2)
                nc.vector.tensor_tensor(gbi[:, :], vec[:, V_GNB:V_GNB + CC], gms[:, :], ALU.subtract).then_inc(aff, 1)

            def split_x(i, c):
                dve.wait_ge(xn_ready, 2 * i + c + 1)
                wait(dve, filled["qk"], 8 * i)
                nc.vector.tensor_tensor(x_lo[:, c, :], xin[:, c, :], x_hi[:, c, :].bitcast(F32),
                                        ALU.subtract).then_inc(xsplit_ready, 1)

            def max_reduce(i, b, m):
                n = 64 * i + 16 * b + m + 1
                dve.wait_ge(max_filled, n)
                nc.vector.reduce_max(mx[:, b % 2, m // 2, m % 2:m % 2 + 1], MS[:, m % 2, :], AX.X).then_inc(max_read, 1)
                if m == 15:
                    dve.wait_ge(max_read, n)
                    wait(dve, filled["row"], BLOCKS * i + b)
                    nc.vector.tensor_tensor(mx1[:, :], mx[:, b % 2, :, 0], mx[:, b % 2, :, 1], ALU.max).then_inc(max_ready, 1)

            def row(i, b):
                wait(dve, rows_loaded, 32 * (BLOCKS * i + b))
                nc.vector.tensor_copy(mrow[:, :], SB[0:2 * QT, 0:P]).then_inc(read["row"], 1)

            def job(kind, i, f, bank=SB[:, :]):
                if kind in ("gna", "gnb", "proj", "router", "conv3", "row", "bias"):
                    dve.wait_ge(filled[kind], done(kind, i, f))
                if kind == "gna":
                    nc.vector.reduce_sum(gsum[:, :, :], bank[:, 0:CC * SUBSETS * 3].rearrange("p (c s k) -> p c k s", c=CC, k=3),
                                         AX.X).then_inc(read["gna"], 1)
                    dve.wait_ge(read["gna"], i + 1)
                    for c in range(CC):
                        last = nc.vector.tensor_scalar(gdev[:, c, :], bst[:, c, :, 1], gsum[:, c, 1:2], None, ALU.subtract)
                    last.then_inc(dev_done, 1)
                    nc.vector.tensor_scalar(gvar_in[:, :], gsum[:, :, 2], SUBSETS / N, EPS, ALU.mult, ALU.add).then_inc(gvar_part, 1)
                    dve.wait_ge(dev_done, i + 1)
                    nc.vector.tensor_tensor(gdev2[:, :, :], gdev[:, :, :], gdev[:, :, :], ALU.mult).then_inc(dev2_ready, 1)
                elif kind == "row":
                    row(i, f)
                elif kind == "bias":
                    nc.vector.tensor_tensor(pbias[:, :], bank[:, 0:CC], vec[:, V_PROJB:V_PROJB + CC], ALU.add).then_inc(read["bias"], 1)
                elif kind == "gnb":
                    nc.vector.reduce_sum(gvar_of[:, :], bank[:, 0:CC * SUBSETS].rearrange("p (c s) -> p c s", c=CC),
                                         AX.X).then_inc(read["gnb"], 1)
                    dve.wait_ge(read["gnb"], i + 1)
                    dve.wait_ge(gvar_part, i + 1)
                    nc.vector.tensor_tensor(gvar[:, :], gvar_of[:, :], gvar_in[:, :], ALU.add).then_inc(gvar_ready, 1)
                elif kind == "qk":
                    p, isq, hf = f // 4, f % 4 // 2, f % 2
                    hi = Q1 if isq else K1
                    for a in range(2):
                        h = 2 * p + a
                        dve.wait_ge(qk_hi, 2 * (8 * i + f) + a + 1)
                        dst = Q2[own(a), h, px(hf)] if isq else K1[other(a), h, px(hf)]
                        last = nc.vector.tensor_tensor(dst, qk_raw[own(a), f % 2, :], hi[own(a), h, px(hf)].bitcast(F32), ALU.subtract)
                    last.then_inc(qk_lo, 1)
                elif kind == "proj":
                    hf, oc = f // CC, f % CC
                    dve.wait_ge(x2_loaded, 16 * i + 16)
                    nc.vector.scalar_tensor_tensor(out=x2[:, oc, px(hf)], in0=bank, scalar=pbias[:, oc:oc + 1],
                                                   in1=x2[:, oc, px(hf)], op0=ALU.add, op1=ALU.add,
                                                   accum_out=pool4[:, oc, hf:hf + 1]).then_inc(read["proj"], 1)
                    if f == 3:
                        dve.wait_ge(read["proj"], 4 * i + 4)
                        nc.vector.tensor_tensor(pool2[:, :], pool4[:, :, 0], pool4[:, :, 1], ALU.add).then_inc(pool_done, 1)
                        dve.wait_ge(pool_done, 2 * i + 1)
                        for c in range(CC):
                            last = nc.vector.tensor_scalar(poolb[:, c, :], ones[:, :], pool2[:, c:c + 1], None, ALU.mult)
                        last.then_inc(pool_done, 1)
                elif kind == "router":
                    nc.vector.scalar_tensor_tensor(out=logit[:, :], in0=bank[:, 0:E], scalar=1.0 / N, in1=rbias[:, :],
                                                   op0=ALU.mult, op1=ALU.add).then_inc(read["router"], 1)
                elif kind == "conv3":
                    oc, hf = f // NH, f % NH
                    if f >= YBUF:
                        wait(dve, y_stored[f - YBUF], 16 * i + 16)
                    else:
                        wait(dve, y_stored[f + YBUF if f + YBUF < 4 else f], 16 * i)
                    nc.vector.scalar_tensor_tensor(out=y[:, f % YBUF, :], in0=bank, scalar=bn_s[:, 2 + oc:3 + oc],
                                                   in1=x2[:, oc, px(hf)], op0=ALU.mult, op1=ALU.add).then_inc(read["conv3"], 1)

            def reciprocal(i, f, part):
                cols = slice(part * HALF // 2, (part + 1) * HALF // 2)
                dve.wait_ge(read["z"], 4 * i + f + 1)
                nc.vector.reciprocal(rz[:, f % 2, cols], rz[:, f % 2, cols]).then_inc(rz_ready, 1)

            def normalise_o(i, f):
                reciprocal(i, f, 1)
                dve.wait_ge(rz_ready, 2 * (4 * i + f) + 2)
                dve.wait_ge(o_saved, BLOCKS * i + f + 1)
                wait(dve, filled["proj"], 4 * i)
                nc.vector.tensor_tensor(o[:, f // NH, px(f % NH)], o_raw[:, f % 2, :], rz[:, f % 2, :],
                                        ALU.mult).then_inc(o_norm, 1)

            def gates(i):
                dve.wait_ge(rexp_ready, i + 1)
                nc.vector.tensor_scalar(rden[:, :], rexp[:, :], 1.0, None, ALU.add).then_inc(rw_chain, 1)
                dve.wait_ge(rw_chain, 2 * i + 1)
                nc.vector.reciprocal(rw[:, :], rden[:, :]).then_inc(rw_chain, 1)
                dve.wait_ge(rw_chain, 2 * i + 2)

            def mix_experts(i, e0, e1):
                for e in range(e0, e1):
                    if e == 0:
                        gates(i)
                        wait(dve, filled["conv3"], 4 * i)
                        nc.vector.tensor_scalar(mix[:, :], ex[:, 0, :], rw[:, 0:1], None, ALU.mult).then_inc(mix_chain, 1)
                    else:
                        dve.wait_ge(mix_chain, E * i + e)
                        nc.vector.scalar_tensor_tensor(out=mix[:, :], in0=ex[:, e, :], scalar=rw[:, e:e + 1], in1=mix[:, :],
                                                       op0=ALU.mult, op1=ALU.add).then_inc(mix_chain, 1)
                    if e == E - 1:
                        dve.wait_ge(mix_chain, E * i + E)
                        for hf in range(NH):
                            last = nc.vector.tensor_copy(mix3[own(hf), hf, :], mix[own(hf), M1 + M2:MIX])
                        last.then_inc(mix_ready, 1)

            def mix_last(i):
                gates(i)
                n = E * i
                for c0, c1 in ((0, M1), (M1, M1 + M2), (M1 + M2, MIX)):
                    for e in range(E):
                        if e == 0:
                            if c0 == 0:
                                dve.wait_ge(filled["conv3"], 4 * i)
                            op = nc.vector.tensor_scalar(mix[:, c0:c1], ex[:, 0, c0:c1], rw[:, 0:1], None, ALU.mult)
                        else:
                            dve.wait_ge(mix_chain, n)
                            op = nc.vector.scalar_tensor_tensor(out=mix[:, c0:c1], in0=ex[:, e, c0:c1], scalar=rw[:, e:e + 1],
                                                                in1=mix[:, c0:c1], op0=ALU.mult, op1=ALU.add)
                        if c0 == 0 and e == E - 1:
                            op.then_inc(mix_ready, 1)
                        elif c0 == M1 and e == E - 1:
                            op.then_inc(mix_rest_ready, 1)
                        else:
                            op.then_inc(mix_chain, 1)
                            n += 1
                dve.wait_ge(mix_chain, n)
                for hf in range(NH):
                    last = nc.vector.tensor_copy(mix3[own(hf), hf, :], mix[own(hf), M1 + M2:MIX])
                last.then_inc(mix_rest_ready, 1)

            dve.wait_ge(norm_loaded, 32)
            nc.vector.tensor_scalar(bn_var[:, :], vec[:, V_V:V_V + 4], EPS, None, ALU.add).then_inc(dve_set, 1)
            for c in range(CC):
                stats(0, c)
            turns = in_turn(PROLOGUE, len(BANKS))
            for kind, f, bank, _ in turns[:BEFORE_PAIRS]:
                job(kind, 0, f, bank)
                if kind == "gnb":
                    affine(0)
                    dve.wait_ge(w_hi_ready, 1)
                    nc.vector.tensor_tensor(w_lo[:, :, :], w_stage, w_hi[:, :, :].bitcast(F32), ALU.subtract).then_inc(dve_set, 1)
                    split_x(0, 0)
                    split_x(0, 1)
            dve.wait_ge(bn_pow, 1)
            nc.vector.tensor_tensor(bn_s[:, :], bn_rs[:, :], vec[:, V_G:V_G + 4], ALU.mult).then_inc(dve_set, 1)
            dve.wait_ge(dve_set, 3)
            nc.vector.tensor_tensor(bn_ms[:, :], bn_s[:, :], vec[:, V_M:V_M + 4], ALU.mult).then_inc(dve_set, 1)
            dve.wait_ge(dve_set, 4)
            nc.vector.tensor_tensor(bn_c[:, :], vec[:, V_B:V_B + 4], bn_ms[:, :], ALU.subtract).then_inc(dve_set, 1)
            for n in range(FIRST_PAIRS):
                b, m = n // 8, 2 * n % 16
                dve.wait_ge(max_filled, 2 * n + 2)
                nc.vector.reduce_max(mx[:, b, m // 2, :], PAIR_BANKS[n % 3], AX.X).then_inc(max_read, 2)
                if n == 7:
                    dve.wait_ge(max_read, 16)
                    nc.vector.tensor_tensor(mx1[:, :], mx[:, 0, :, 0], mx[:, 0, :, 1], ALU.max).then_inc(max_ready, 1)
                if n - 1 in JOB_AFTER_PAIR:
                    kind, f, bank, _ = turns[BEFORE_PAIRS + JOB_AFTER_PAIR.index(n - 1)]
                    job(kind, 0, f, bank)
                if n == 8:
                    job("row", 0, 0)
            dve.wait_ge(consts_set, CONSTS_SET)
            dve.wait_ge(rest_loaded, 16 * 5)

            def section(i, first, last):
                mixed = 0
                for s in range(STEPS):
                    fills = fills_at(i, s, last)
                    jobs = jobs_of(s, first, last)
                    slow = [j for j in jobs if j[0] == "qk" or is_second(s, j)]
                    for at in fills[0:1]:
                        max_reduce(*at)
                    for kind, di, f in jobs:
                        if (kind, di, f) not in slow:
                            job(kind, i + di, f)
                    for at in fills[1:2]:
                        max_reduce(*at)
                    for kind, di, f in slow:
                        job(kind, i + di, f)
                    for at in fills[2:]:
                        max_reduce(*at)
                    if s in NORMALISE and not (first and NORMALISE[s][0] < 0):
                        di, f = NORMALISE[s]
                        reciprocal(i + di, f, 0)
                    if s - 1 in NORMALISE and not (first and NORMALISE[s - 1][0] < 0):
                        di, f = NORMALISE[s - 1]
                        normalise_o(i + di, f)
                    if s in STATS_STEPS and not last:
                        stats(i + 1, STATS_STEPS.index(s))
                    if s == AFFINE_STEP and not last:
                        affine(i + 1)
                    if s in SPLIT_STEPS and not last:
                        split_x(i + 1, SPLIT_STEPS.index(s))
                    if s in MIX_STEPS and not first:
                        mix_experts(i - 1, mixed, mixed + MIX_STEPS[s])
                        mixed += MIX_STEPS[s]

            sections(dve, section)
            for kind, f, bank, _ in in_turn(EPILOGUE):
                job(kind, B - 1, f, bank)
                if kind == "z":
                    reciprocal(B - 1, f, 0)
                    normalise_o(B - 1, f)
                if kind == "router":
                    mix_last(B - 1)


_ORDER = ["x", "vecs", "router_b", "wqkv", "wproj", "wrouter", "experts", "neg_eye", "group_avg"]


def _chunks(v):
    return np.asarray(v).reshape(-1, P).T


def kernel(**inputs):
    import concourse.bacc as _bacc
    from concourse.bass_utils import run_bass_kernel_spmd as _run

    a = {k: np.asarray(v) for k, v in inputs.items()}
    c1 = {k[len("L1_conv_"):]: v for k, v in a.items() if k.startswith("L1_conv_")}

    def layers(k):
        return np.concatenate([np.tile(c1[k + "1"], 2)[:, None], np.tile(c1[k + "2"], 2)[:, None], _chunks(c1[k + "3"])], axis=1)

    vecs = np.concatenate([_chunks(a["L0_conv_gn_w"]), _chunks(a["L0_conv_gn_b"]), _chunks(a["L0_conv_qkv_b"]),
                           _chunks(a["L0_conv_proj_b"]), layers("g"), layers("b"), layers("m"), layers("v")], axis=1)

    def stationary(w):
        return w.T.reshape(CC, P, -1).transpose(1, 0, 2)

    e1 = c1["w1"][:, :, :, 0, 0].transpose(2, 0, 1).reshape(CC, P, E, WID).transpose(1, 2, 0, 3).reshape(P, E, M1)
    w2 = c1["w2"].transpose(4, 2, 0, 3, 1)
    low = np.concatenate([w2[0], w2[2]], axis=2)
    high = np.concatenate([w2[1], np.zeros_like(w2[1])], axis=2)
    e2 = np.concatenate([low, high], axis=0).reshape(P, E, M2)
    w3 = c1["w3"][:, :, :, 0, 0].transpose(2, 0, 1)
    e3 = np.concatenate([w3, w3], axis=0)
    arrays = {
        "x": a["x"].reshape(B, CC, P, N),
        "vecs": vecs,
        "router_b": np.broadcast_to(c1["router_b"], (P, E)),
        "wqkv": stationary(a["L0_conv_qkv_w"]),
        "wproj": stationary(a["L0_conv_proj_w"]),
        "wrouter": stationary(c1["router_w"]),
        "experts": np.concatenate([e1, e2, e3], axis=2),
        "neg_eye": -np.eye(P, dtype=np.float32),
        "group_avg": np.kron(np.eye(P // GROUP, dtype=np.float32), np.full((GROUP, GROUP), 1 / (GROUP * SUBSETS), np.float32)),
    }
    nc = _bacc.Bacc("TRN2", target_bir_lowering=False, num_devices=1)
    data, args = {}, []
    for name in _ORDER:
        v = np.ascontiguousarray(arrays[name])
        data[f"in_{name}_dram"] = v
        ap = nc.dram_tensor(f"in_{name}_dram", v.shape, mybir.dt.from_np(v.dtype), kind="ExternalInput").ap()
        args.append(ap.rearrange("b c p n -> b p c n") if name == "x" else ap)
    res = nc.dram_tensor("out_0_dram", (B, CC, P, N), F32, kind="ExternalOutput").ap()
    build(nc, *args, res.rearrange("b c p n -> b p c n"))
    r = _run(nc, [data], core_ids=[0])
    return r.results[0]["out_0_dram"].reshape(B, C, H, W)
```
